# Optimizing a Trainium2 kernel written in Bass

```python
import numpy as np
import jax
import jax.numpy as jnp

def _softmax(x, axis=-1):
    return jax.nn.softmax(x, axis=axis)

def _gelu(x):
    return jax.nn.gelu(x, approximate=True)

def _silu(x):
    return jax.nn.silu(x)

def _sigmoid(x):
    return jax.nn.sigmoid(x)

def _layernorm(x, axis=-1, eps=1e-05):
    m = jnp.mean(x, axis=axis, keepdims=True)
    v = jnp.var(x, axis=axis, keepdims=True)
    return (x - m) / jnp.sqrt(v + eps)

def _scatter_add(tgt, idx, src, axis=0):
    return tgt.at[idx].add(src)

def _segment_sum(src, seg, n):
    return jax.ops.segment_sum(src, seg, n)
kernel_name = 'mk_vit_tower_postln_d1_tok_img512_r4_b3beee'

def setup_inputs(seed: int=0):
    np.random.seed(seed)
    _w = jnp.asarray

    def _rec_inputs():
        import jax
        import jax.numpy as jnp
        _rk = jax.random.key(seed)
        x = 7.57192e-06 + 1.00007 * jax.random.normal(jax.random.fold_in(_rk, 1), (128, 64, 64, 3), jnp.float32)
        return x
    x = _rec_inputs()

    def _L0_tok_setup():
        import jax, jax.numpy as jnp
        import numpy as np
        B, H, W, C = (64, 224, 224, 3)
        P, D = (16, 128)
        LN_EPS = 0.001

        def _shift4(x):
            pad = lambda a, spec: jnp.pad(a, spec)
            right = pad(x[:, :, :-1, :], ((0, 0), (0, 0), (1, 0), (0, 0)))
            left = pad(x[:, :, 1:, :], ((0, 0), (0, 0), (0, 1), (0, 0)))
            down = pad(x[:, :-1, :, :], ((0, 0), (1, 0), (0, 0), (0, 0)))
            up = pad(x[:, 1:, :, :], ((0, 0), (0, 1), (0, 0), (0, 0)))
            return [right, left, down, up]
        key = jax.random.key(seed)
        k0, k1, k2 = jax.random.split(key, 3)
        x = jax.random.normal(k0, (B, H, W, C), jnp.float32)
        conv_w = jax.random.normal(k1, (P, P, 5 * C, D), jnp.float32) * 0.02
        conv_b = jnp.zeros((D,), jnp.float32)
        gamma = jnp.ones((D,), jnp.float32)
        beta = jnp.zeros((D,), jnp.float32)
        dense_w = jax.random.normal(k2, (D, D), jnp.float32) * 0.02
        dense_b = jnp.zeros((D,), jnp.float32)
        return {'x': x, 'conv_w': conv_w, 'conv_b': conv_b, 'gamma': gamma, 'beta': beta, 'dense_w': dense_w, 'dense_b': dense_b}
    _L0_tok_all = _L0_tok_setup()
    _L0_tok_in = {k: v for k, v in _L0_tok_all.items() if k in ('conv_w', 'conv_b', 'gamma', 'beta', 'dense_w', 'dense_b')}
    del _L0_tok_all

    def _L0_attn_setup():
        import jax, jax.numpy as jnp
        import numpy as np
        B, L, D, H = (2, 1024, 128, 8)
        DK = D // H
        SCALE = 1.0 / float(np.sqrt(DK))
        key = jax.random.key(seed)
        k1, k2, k3 = jax.random.split(key, 3)
        x = jax.random.normal(k1, (B, L, D), dtype=jnp.float32)
        w_qkv = jax.random.normal(k2, (3 * D, D), dtype=jnp.float32) * 0.02
        w_o = jax.random.normal(k3, (D, D), dtype=jnp.float32) * 0.02
        return {'x': x, 'w_qkv': w_qkv, 'w_o': w_o}
    _L0_attn_all = _L0_attn_setup()
    _L0_attn_in = {k: v for k, v in _L0_attn_all.items() if k in ('w_qkv', 'w_o')}
    del _L0_attn_all

    def _L0_ffn_setup():
        import jax, jax.numpy as jnp
        import numpy as np
        G = 4
        EPG = 4
        E = 16
        KG = 2
        K = 2
        GTP = 0.9
        TP = 0.9
        SCALE = 1.0 / float(np.sqrt(G))

        def _routing_weights(xf, Wr, br, Wgate, bgate):
            N = xf.shape[0]
            gp = jax.nn.softmax(xf @ Wr + br, axis=-1)
            order = jnp.argsort(-gp, axis=-1)
            sp_k = jnp.take_along_axis(gp, order, axis=-1)[:, :KG]
            idx_k = order[:, :KG]
            act = jnp.cumsum(sp_k, axis=-1) <= GTP
            act = act.at[:, 0].set(True)
            mp = sp_k * act
            rn = mp / (jnp.sum(mp, axis=-1, keepdims=True) + 1e-09)
            w_group = jnp.zeros((N, G), xf.dtype).at[jnp.arange(N)[:, None], idx_k].set(rn)
            ep = jax.nn.softmax(jnp.einsum('nd,gde->nge', xf, Wgate) + bgate, axis=-1)
            eorder = jnp.argsort(-ep, axis=-1)
            esp = jnp.take_along_axis(ep, eorder, axis=-1)[:, :, :K]
            eidx = eorder[:, :, :K]
            eact = jnp.cumsum(esp, axis=-1) <= TP
            eact = eact.at[:, :, 0].set(True)
            emp = esp * eact
            ern = emp / (jnp.sum(emp, axis=-1, keepdims=True) + 1e-09)
            w_exp = jnp.zeros((N, G, EPG), xf.dtype).at[jnp.arange(N)[:, None, None], jnp.arange(G)[None, :, None], eidx].set(ern)
            return (w_group[:, :, None] * w_exp * SCALE).reshape(N, E)
        key = jax.random.key(seed)
        ks = jax.random.split(key, 6)
        B, T, D, H = (2, 256, 128, 512)
        x = jax.random.normal(ks[0], (B, T, D), jnp.float32)
        Wr = jax.random.normal(ks[1], (D, G), jnp.float32) * 0.02
        br = jnp.zeros((G,), jnp.float32)
        Wgate = jax.random.normal(ks[2], (G, D, EPG), jnp.float32) * 0.02
        bgate = jnp.zeros((G, EPG), jnp.float32)
        W1 = jax.random.normal(ks[3], (E, D, H), jnp.float32) * 0.02
        W3 = jax.random.normal(ks[4], (E, D, H), jnp.float32) * 0.02
        W2 = jax.random.normal(ks[5], (E, H, D), jnp.float32) * 0.02
        return {'x': x, 'Wr': Wr, 'br': br, 'Wgate': Wgate, 'bgate': bgate, 'W1': W1, 'W3': W3, 'W2': W2}
    _L0_ffn_all = _L0_ffn_setup()
    _L0_ffn_in = {k: v for k, v in _L0_ffn_all.items() if k in ('Wr', 'br', 'Wgate', 'bgate', 'W1', 'W3', 'W2')}
    del _L0_ffn_all
    return {'x': x, 'L0_tok_conv_w': _L0_tok_in['conv_w'], 'L0_tok_conv_b': _L0_tok_in['conv_b'], 'L0_tok_gamma': _L0_tok_in['gamma'], 'L0_tok_beta': _L0_tok_in['beta'], 'L0_tok_dense_w': _L0_tok_in['dense_w'], 'L0_tok_dense_b': _L0_tok_in['dense_b'], 'L0_attn_w_qkv': _L0_attn_in['w_qkv'], 'L0_attn_w_o': _L0_attn_in['w_o'], 'L0_ffn_Wr': _L0_ffn_in['Wr'], 'L0_ffn_br': _L0_ffn_in['br'], 'L0_ffn_Wgate': _L0_ffn_in['Wgate'], 'L0_ffn_bgate': _L0_ffn_in['bgate'], 'L0_ffn_W1': _L0_ffn_in['W1'], 'L0_ffn_W3': _L0_ffn_in['W3'], 'L0_ffn_W2': _L0_ffn_in['W2']}

def reference(x, L0_tok_conv_w, L0_tok_conv_b, L0_tok_gamma, L0_tok_beta, L0_tok_dense_w, L0_tok_dense_b, L0_attn_w_qkv, L0_attn_w_o, L0_ffn_Wr, L0_ffn_br, L0_ffn_Wgate, L0_ffn_bgate, L0_ffn_W1, L0_ffn_W3, L0_ffn_W2):
    import jax
    import jax.numpy as jnp

    def _L0_tok_ref(x, conv_w, conv_b, gamma, beta, dense_w, dense_b):
        import jax, jax.numpy as jnp
        import numpy as np
        B, H, W, C = (64, 224, 224, 3)
        P, D = (16, 128)
        LN_EPS = 0.001

        def _shift4(x):
            pad = lambda a, spec: jnp.pad(a, spec)
            right = pad(x[:, :, :-1, :], ((0, 0), (0, 0), (1, 0), (0, 0)))
            left = pad(x[:, :, 1:, :], ((0, 0), (0, 0), (0, 1), (0, 0)))
            down = pad(x[:, :-1, :, :], ((0, 0), (1, 0), (0, 0), (0, 0)))
            up = pad(x[:, 1:, :, :], ((0, 0), (0, 1), (0, 0), (0, 0)))
            return [right, left, down, up]
        xs = jnp.concatenate([x, *_shift4(x)], axis=-1)
        y = jax.lax.conv_general_dilated(xs, conv_w, window_strides=(P, P), padding='VALID', dimension_numbers=('NHWC', 'HWIO', 'NHWC')) + conv_b
        y = y.reshape(y.shape[0], -1, D)
        mu = jnp.mean(y, axis=-1, keepdims=True)
        var = jnp.mean(jnp.square(y - mu), axis=-1, keepdims=True)
        y = (y - mu) * jax.lax.rsqrt(var + LN_EPS) * gamma + beta
        return y @ dense_w + dense_b

    def _L0_attn_ref(x, w_qkv, w_o):
        import jax, jax.numpy as jnp
        import numpy as np
        B, L, D, H = (2, 1024, 128, 8)
        DK = D // H
        SCALE = 1.0 / float(np.sqrt(DK))
        b, l, d = x.shape
        qkv = (x @ w_qkv.T).reshape(b, l, 3, H, DK).transpose(2, 0, 3, 1, 4)
        q, k, v = (qkv[0], qkv[1], qkv[2])
        scores = jnp.einsum('bhld,bhmd->bhlm', q, k) * SCALE
        attn = jax.nn.softmax(scores, axis=-1)
        ctx = jnp.einsum('bhlm,bhmd->bhld', attn, v)
        ctx = ctx.transpose(0, 2, 1, 3).reshape(b, l, d)
        return ctx @ w_o.T

    def _L0_ffn_ref(x, Wr, br, Wgate, bgate, W1, W3, W2):
        import jax, jax.numpy as jnp
        import numpy as np
        G = 4
        EPG = 4
        E = 16
        KG = 2
        K = 2
        GTP = 0.9
        TP = 0.9
        SCALE = 1.0 / float(np.sqrt(G))

        def _routing_weights(xf, Wr, br, Wgate, bgate):
            N = xf.shape[0]
            gp = jax.nn.softmax(xf @ Wr + br, axis=-1)
            order = jnp.argsort(-gp, axis=-1)
            sp_k = jnp.take_along_axis(gp, order, axis=-1)[:, :KG]
            idx_k = order[:, :KG]
            act = jnp.cumsum(sp_k, axis=-1) <= GTP
            act = act.at[:, 0].set(True)
            mp = sp_k * act
            rn = mp / (jnp.sum(mp, axis=-1, keepdims=True) + 1e-09)
            w_group = jnp.zeros((N, G), xf.dtype).at[jnp.arange(N)[:, None], idx_k].set(rn)
            ep = jax.nn.softmax(jnp.einsum('nd,gde->nge', xf, Wgate) + bgate, axis=-1)
            eorder = jnp.argsort(-ep, axis=-1)
            esp = jnp.take_along_axis(ep, eorder, axis=-1)[:, :, :K]
            eidx = eorder[:, :, :K]
            eact = jnp.cumsum(esp, axis=-1) <= TP
            eact = eact.at[:, :, 0].set(True)
            emp = esp * eact
            ern = emp / (jnp.sum(emp, axis=-1, keepdims=True) + 1e-09)
            w_exp = jnp.zeros((N, G, EPG), xf.dtype).at[jnp.arange(N)[:, None, None], jnp.arange(G)[None, :, None], eidx].set(ern)
            return (w_group[:, :, None] * w_exp * SCALE).reshape(N, E)
        B, T, D = x.shape
        xf = x.reshape(-1, D)
        tw = _routing_weights(xf, Wr, br, Wgate, bgate)
        out = jnp.zeros_like(xf)
        for e in range(E):
            h = jax.nn.silu(xf @ W1[e]) * (xf @ W3[e])
            out = out + tw[:, e:e + 1] * (h @ W2[e])
        return out.reshape(B, T, D)
    h = _L0_tok_ref(x, L0_tok_conv_w, L0_tok_conv_b, L0_tok_gamma, L0_tok_beta, L0_tok_dense_w, L0_tok_dense_b)
    h = _layernorm(h + _L0_attn_ref(h, L0_attn_w_qkv, L0_attn_w_o), axis=-1)
    h = _layernorm(h + _L0_ffn_ref(h, L0_ffn_Wr, L0_ffn_br, L0_ffn_Wgate, L0_ffn_bgate, L0_ffn_W1, L0_ffn_W3, L0_ffn_W2), axis=-1)
    return h

_drawn_inputs = setup_inputs


def setup_inputs(seed=0):
    import zlib

    import numpy as np

    out = dict(_drawn_inputs(seed))
    spreads = {'L0_tok_conv_b': (0.0, 0.1),
     'L0_tok_gamma': (1.0, 0.2),
     'L0_tok_beta': (0.0, 0.1),
     'L0_tok_dense_b': (0.0, 0.1),
     'L0_ffn_br': (0.0, 0.8),
     'L0_ffn_bgate': (0.0, 0.8)}
    factors = {'L0_attn_w_qkv': 2.738,
     'L0_ffn_Wr': 8.0,
     'L0_ffn_Wgate': 8.0,
     'L0_ffn_W1': 8.0,
     'L0_ffn_W3': 8.0,
     'L0_ffn_W2': 8.0}
    for name, (base, spread) in spreads.items():
        noise = np.random.default_rng([zlib.crc32(name.encode()), seed]).standard_normal(out[name].shape)
        drawn = base * np.exp(spread * noise) if base else spread * noise
        out[name] = jnp.asarray(drawn.astype(out[name].dtype))
    for name, factor in factors.items():
        out[name] = (out[name] * factor).astype(out[name].dtype)
    return out
```

```python
from contextlib import ExitStack

import concourse.bass as bass
from concourse import mybir

ALU = mybir.AluOpType
ACT = mybir.ActivationFunctionType
AX = mybir.AxisListType
F32 = mybir.dt.float32

P = 128
D = 128
TOKENS = 2048
QT = 512
NQ = TOKENS // QT
TPQ = QT // P
IMG = 16
IPQ = QT // IMG
HEADS = 8
DK = D // HEADS
SCALE = DK ** -0.5
G = 4
EPG = 4
E = G * EPG
GR = G + 1
HID = 512
HC = HID // P
TILES = TOKENS // P
CH = 8
RIM = 96
TOK_EPS = 1e-3
LN_EPS = 1e-5


def build_program(nc, xmain, xrim, taps, wrim, conv_b, gamma, beta, dense_w, dense_b, wqkv_t,
                  wo_t, wroute, broute, w1, w3, w2, out):
    ctx = ExitStack()
    with ctx:
        def sb(name, shape):
            return ctx.enter_context(nc.sbuf_tensor(name, shape, F32))

        def sem(name):
            return ctx.enter_context(nc.semaphore(name))

        bank = [ctx.enter_context(nc.psum_tensor(f"bank{i}", [P, 512], F32)) for i in range(8)]
        CONV, TOKM, NORM, H0T, QB, KB, VB, ST = bank
        VT = [NORM, H0T]
        SC, PT, CTX, ATT = QB, KB, VB, TOKM
        X1T, LG = QB, KB

        ident = sb("ident", [P, P])
        tapsum = sb("tapsum", [P, 5, 6, D])
        wconv = sb("wconv", [P, CH, D])
        convb = sb("convb", [P, 1])
        gam = sb("gam", [P, 1])
        bet = sb("bet", [P, 1])
        dw = sb("dw", [P, D])
        dbcol = sb("dbcol", [P, 1])
        dbrow = sb("dbrow", [P, D])
        wqkv = sb("wqkv", [P, 3 * D])
        wo = sb("wo", [P, D])
        wr = sb("wr", [P, GR * 4])
        br = sb("br", [P, GR * 4])
        mhalf = sb("mhalf", [P, TPQ])
        tril = sb("tril", [P, 4, 4])
        xcol = sb("xcol", [P, 2, CH, QT])
        ycT = sb("ycT", [P, QT])
        st6 = sb("st6", [P, TPQ, 6])
        mv = sb("mv", [P, TPQ, 2])
        rstd = sb("rstd", [P, TPQ])
        st6b = sb("st6b", [P, TPQ, 6])
        mvb = sb("mvb", [P, TPQ, 2])
        rstdb = sb("rstdb", [P, TPQ])
        veps = sb("veps", [P, TPQ])
        vepsb = sb("vepsb", [P, TPQ])
        yn = sb("yn", [P, TPQ, D])
        yT = sb("yT", [P, QT])
        h0 = sb("h0", [P, TPQ, D])
        h0T = sb("h0T", [P, QT])
        qT = sb("qT", [P, QT])
        kT = sb("kT", [P, QT])
        vT = sb("vT", [P, QT])
        kblk = sb("kblk", [P, HEADS, QT])
        vblkT = sb("vblkT", [P, HEADS, QT])
        vblk = sb("vblk", [P, IPQ, D])
        sT = sb("sT", [P, QT])
        sc = sb("sc", [P, TPQ * HEADS, IMG])
        pe_ = sb("probs", [P, TPQ * HEADS, IMG])
        pn = sb("pn", [P, TPQ * HEADS, IMG])
        smax = sb("smax", [P, TPQ * HEADS])
        ssum = sb("ssum", [P, TPQ * HEADS])
        srec = sb("srec", [P, TPQ * HEADS])
        pT = sb("pT", [P, QT])
        ctxT = sb("ctxT", [P, QT])
        res = sb("res", [P, TPQ, D])
        x1 = sb("x1", [P, TILES, D])
        x1T = sb("x1T", [P, TILES * P])
        R = TPQ * GR
        lg = sb("lg", [P, R, 4])
        lmax = sb("lmax", [P, R])
        lsh = sb("lsh", [P, R, 4])
        lex = sb("lex", [P, R, 4])
        lsum = sb("lsum", [P, R])
        lrec = sb("lrec", [P, R])
        gp = sb("gp", [P, R, 4])
        gt = sb("gt", [P, R, 4, 4])
        eq = sb("eq", [P, R, 4, 4])
        eqt = sb("eqt", [P, R, 4, 4])
        gte = sb("gte", [P, R, 4, 4])
        rank = sb("rank", [P, R, 4])
        first = sb("first", [P, R, 4])
        second = sb("second", [P, R, 4])
        psec = sb("psec", [P, R, 4])
        p1 = sb("p1", [P, R])
        p2 = sb("p2", [P, R])
        cum = sb("cum", [P, R])
        keep2 = sb("keep2", [P, R])
        kept = sb("kept", [P, R, 4])
        mask = sb("mask", [P, R, 4])
        mp = sb("mp", [P, R, 4])
        msum = sb("msum", [P, R])
        mrec = sb("mrec", [P, R])
        wn = sb("wn", [P, R, 4])
        tw = sb("tw", [P, TILES, G, EPG])
        w1s = sb("w1s", [P, 2, HID])
        w3s = sb("w3s", [P, 2, HID])
        w2s = sb("w2s", [P, 2, HC, D])
        act = sb("act_", [P, 2, HID])
        gu = sb("gu", [P, 2, HC, P])
        guT = sb("guT", [P, 2, HC, P])
        acc = sb("acc", [P, TILES, D])

        dma_w = sem("dma_w")
        dma_c = sem("dma_c")
        x_in = [sem("x_in0"), sem("x_in1")]
        zeros = sem("zeros")
        ident_ok = sem("ident_ok")
        pool_c = sem("pool_c")
        wconv_ok = sem("wconv_ok")
        conv_ok = sem("conv_ok")
        yct_ok = sem("yct_ok")
        ytok_ok = sem("ytok_ok")
        var_ok = sem("var_ok")
        rstd_ok = sem("rstd_ok")
        yn_ok = sem("yn_ok")
        ynt_ok = sem("ynt_ok")
        yt_ok = sem("yt_ok")
        h0_ps = sem("h0_ps")
        h0t_ps = sem("h0t_ps")
        h0_ok = sem("h0_ok")
        h0t_ok = sem("h0t_ok")
        q_ps = sem("q_ps")
        k_ps = sem("k_ps")
        v_ps = sem("v_ps")
        q_ok = sem("q_ok")
        k_ok = sem("k_ok")
        v_ok = sem("v_ok")
        kblk_in = sem("kblk_in")
        vblk_in = sem("vblk_in")
        vt_ps = sem("vt_ps")
        vt_act = sem("vt_act")
        vt_dve = sem("vt_dve")
        st_ps = sem("st_ps")
        st_ok = sem("st_ok")
        sc_ps = sem("sc_ps")
        sh_ok = sem("sh_ok")
        exp_ok = sem("exp_ok")
        pn_ok = sem("pn_ok")
        pt_ps = sem("pt_ps")
        pt_ok = sem("pt_ok")
        ctx_ps = sem("ctx_ps")
        ctx_ok = sem("ctx_ok")
        att_ps = sem("att_ps")
        x1_ok = sem("x1_ok")
        x1t_ps = sem("x1t_ps")
        x1t_ok = sem("x1t_ok")
        lg_ps = sem("lg_ps")
        lsh_ok = sem("lsh_ok")
        lex_ok = sem("lex_ok")
        pool_s = sem("pool_s")
        dve_s = sem("dve_s")
        w_in = [sem("w_in0"), sem("w_in1")]
        up_ps = sem("up_ps")
        act_ok = sem("act_ok")
        gu_ok = sem("gu_ok")
        gut_ps = sem("gut_ps")
        gut_ok = sem("gut_ok")
        y_ps = sem("y_ps")
        acc_ok = sem("acc_ok")
        fin_ok = sem("fin_ok")
        out_done = sem("out_done")

        NSTEPS = E * TILES
        N_CONST = 12
        block = ctx.enter_context(nc.Block())

        @block.sync
        def _(sp):
            sp.dma_start(tapsum[:, :, :, :], taps).then_inc(dma_w, 16)
            sp.dma_start(wconv[0:RIM, 6:8, :], wrim).then_inc(dma_w, 16)

            def load_x(q, slot):
                sp.dma_start(xcol[:, slot, 0:6, :], xmain[q]).then_inc(x_in[slot], 16)
                sp.dma_start(xcol[0:RIM, slot, 6:8, :], xrim[q]).then_inc(x_in[slot], 16)

            load_x(0, 0)
            load_x(1, 1)

            def blocks(q):
                sp.wait_ge(zeros, 2)
                sp.wait_ge(k_ok, q + 1)
                sp.wait_ge(st_ps, q)
                for h in range(HEADS):
                    sp.dma_start(kblk[DK * h:DK * (h + 1), h, :],
                                 kT[DK * h:DK * (h + 1), :]).then_inc(kblk_in, 16)
                sp.wait_ge(v_ok, q + 1)
                sp.wait_ge(vt_ps, 8 * q)
                for h in range(HEADS):
                    sp.dma_start(vblkT[DK * h:DK * (h + 1), h, :],
                                 vT[DK * h:DK * (h + 1), :]).then_inc(vblk_in, 16)

            for q in range(NQ):
                if q + 2 < NQ:
                    sp.wait_ge(conv_ok, q + 1)
                    load_x(q + 2, q % 2)
                blocks(q)

            for e in range(E):
                if e >= 2:
                    sp.wait_ge(y_ps, (e - 1) * TILES)
                s = e % 2
                sp.dma_start(w1s[:, s, :], w1[e]).then_inc(w_in[s], 16)
                sp.dma_start(w3s[:, s, :], w3[e]).then_inc(w_in[s], 16)
                sp.dma_start(w2s[:, s, :, :], w2[e]).then_inc(w_in[s], 16)
            sp.wait_ge(fin_ok, TILES)
            sp.dma_start(out, acc[:, :, :]).then_inc(out_done, 16)
            sp.wait_ge(out_done, 16)

        @block.gpsimd
        def _(pool):
            pool.memset(ident[:, :], 0.0).then_inc(pool_c, 1)
            pool.wait_ge(pool_c, 1)
            pool.affine_select(out=ident[:, :], in_=ident[:, :], compare_op=ALU.not_equal, fill=1.0,
                               base=0, pattern=[[-1, P]], channel_multiplier=1).then_inc(ident_ok, 1)
            pool.memset(mhalf[:, :], -0.5).then_inc(pool_c, 1)
            pool.memset(tril[:, :, :], 1.0).then_inc(pool_c, 1)
            pool.wait_ge(pool_c, 3)
            pool.affine_select(out=tril[:, :, :], in_=tril[:, :, :], compare_op=ALU.is_gt, fill=0.0,
                               base=0, pattern=[[1, 4], [-1, 4]], channel_multiplier=0).then_inc(ident_ok, 1)
            pool.memset(kblk[:, :, :], 0.0).then_inc(zeros, 1)
            pool.memset(vblkT[:, :, :], 0.0).then_inc(zeros, 1)
            steps = [0]

            def rsqrt(dst, tmp, var, eps):
                pool.tensor_scalar(tmp, var, eps, None, ALU.add).then_inc(pool_s, 1)
                steps[0] += 1
                pool.wait_ge(pool_s, steps[0])
                pool.tensor_tensor(dst, tmp, mhalf[:, :], ALU.pow).then_inc(rstd_ok, 1)

            for q in range(NQ):
                pool.wait_ge(var_ok, 2 * q + 1)
                rsqrt(rstd[:, :], veps[:, :], mv[:, :, 1], TOK_EPS)
                pool.wait_ge(var_ok, 2 * q + 2)
                rsqrt(rstdb[:, :], vepsb[:, :], mvb[:, :, 1], LN_EPS)
            for t in range(NQ):
                pool.wait_ge(var_ok, 2 * NQ + t + 1)
                rsqrt(rstdb[:, :], vepsb[:, :], mvb[:, :, 1], LN_EPS)

        @block.scalar
        def _(ac):
            for dst, src in ((convb[:, :], conv_b), (gam[:, :], gamma), (bet[:, :], beta),
                             (dbcol[:, :], dense_b)):
                ac.dma_start(dst, src.rearrange("(p a) -> p a", a=1)).then_inc(dma_c, 16)
            for dst, src in ((dw, dense_w), (wqkv, wqkv_t), (wo, wo_t), (wr, wroute)):
                ac.dma_start(dst[:, :], src).then_inc(dma_c, 16)
            ac.dma_start(dbrow[:, :], dense_b.partition_broadcast(P)).then_inc(dma_c, 16)
            ac.dma_start(br[:, :], broute.partition_broadcast(P)).then_inc(dma_c, 16)
            ac.wait_ge(dma_c, 160)

            def conv_out(q):
                ac.wait_ge(conv_ok, q + 1)
                if q:
                    ac.wait_ge(ytok_ok, q)
                ac.activation(ycT[:, :], CONV[:, :], ACT.Identity, bias=convb[:, 0:1]).then_inc(yct_ok, 1)

            conv_out(0)
            for q in range(NQ):
                ac.wait_ge(ynt_ok, q + 1)
                ac.activation(yT[:, :], NORM[:, :], ACT.Identity, bias=bet[:, 0:1],
                              scale=gam[:, 0:1]).then_inc(yt_ok, 1)
                ac.wait_ge(h0t_ps, q + 1)
                ac.activation(h0T[:, :], H0T[:, :], ACT.Identity, bias=dbcol[:, 0:1]).then_inc(h0t_ok, 1)
                ac.wait_ge(q_ps, q + 1)
                ac.activation(qT[:, :], QB[:, :], ACT.Copy, scale=SCALE).then_inc(q_ok, 1)
                ac.wait_ge(k_ps, q + 1)
                if q:
                    ac.wait_ge(kblk_in, 128 * q)
                ac.activation(kT[:, :], KB[:, :], ACT.Copy).then_inc(k_ok, 1)
                ac.wait_ge(v_ps, q + 1)
                if q:
                    ac.wait_ge(vblk_in, 128 * q)
                ac.activation(vT[:, :], VB[:, :], ACT.Copy).then_inc(v_ok, 1)
                if q + 1 < NQ:
                    conv_out(q + 1)
                ac.wait_ge(st_ps, q + 1)
                ac.activation(sT[:, :], ST[:, :], ACT.Copy).then_inc(st_ok, 1)
                for j in range(4):
                    ac.wait_ge(vt_ps, 8 * q + 2 * j + 1)
                    if q and j == 0:
                        ac.wait_ge(ctx_ps, q)
                    ac.activation(vblk[:, 8 * j:8 * j + 4, :], VT[0][:, :].rearrange("p (i d) -> p i d", d=D),
                                  ACT.Copy).then_inc(vt_act, 1)
                    if j == 1:
                        ac.wait_ge(sh_ok, q + 1)
                        ac.activation(pe_[:, :, :], sc[:, :, :], ACT.Exp).then_inc(exp_ok, 1)
                ac.wait_ge(pt_ps, q + 1)
                ac.activation(pT[:, :], PT[:, :], ACT.Copy).then_inc(pt_ok, 1)
                ac.wait_ge(ctx_ps, q + 1)
                ac.activation(ctxT[:, :].rearrange("p (m i) -> p m i", i=IPQ),
                              CTX[:, :].rearrange("p (i m) -> p m i", i=IPQ), ACT.Copy).then_inc(ctx_ok, 1)
                ac.wait_ge(x1t_ps, q + 1)
                ac.activation(x1T[:, q * QT:(q + 1) * QT], X1T[:, :], ACT.Copy).then_inc(x1t_ok, 1)
                ac.wait_ge(lsh_ok, q + 1)
                ac.activation(lex[:, :, :], lsh[:, :, :], ACT.Exp).then_inc(lex_ok, 1)

            def silu_of(n, s):
                ac.wait_ge(up_ps, n + 1)
                ac.activation(act[:, s, :], bank[2 * s][:, :], ACT.Silu).then_inc(act_ok, 1)

            def gut_of(n, s):
                ac.wait_ge(gut_ps, n + 1)
                ac.activation(guT[:, s, :, :], bank[4 + s][:, :].rearrange("p (c t) -> p c t", t=P),
                              ACT.Copy).then_inc(gut_ok, 1)

            with ac.Fori(0, NSTEPS // 2) as k:
                for s in range(2):
                    silu_of(k * 2 + s, s)
                    gut_of(k * 2 + s, s)

        @block.vector
        def _(dve):
            N_Q = 0
            c = [0]

            def step(inst):
                inst.then_inc(dve_s, 1)
                c[0] += 1

            def settled():
                dve.wait_ge(dve_s, c[0])

            dve.wait_ge(dma_w, 32)
            tp = [tapsum[:, i, :, :] for i in range(5)]
            step(nc.vector.tensor_tensor(wconv[:, 0:6, :], tp[0], tp[1], ALU.add))
            step(nc.vector.tensor_tensor(tp[2], tp[2], tp[3], ALU.add))
            settled()
            step(nc.vector.tensor_tensor(wconv[:, 0:6, :], wconv[:, 0:6, :], tp[4], ALU.add))
            settled()
            nc.vector.tensor_tensor(wconv[:, 0:6, :], wconv[:, 0:6, :], tp[2], ALU.add).then_inc(wconv_ok, 1)
            dve.wait_ge(dma_c, 160)
            dve.wait_ge(ident_ok, 2)

            def stats(src, st, m):
                for t in range(TPQ):
                    step(nc.vector.bn_stats(st[:, t, :], src(t)))
                settled()
                for t in range(TPQ):
                    last = nc.vector.bn_aggr(m[:, t, :], st[:, t, :])
                    if t < TPQ - 1:
                        step(last)
                last.then_inc(var_ok, 1)

            for q in range(NQ):
                dve.wait_ge(ytok_ok, q + 1)
                stats(lambda t: TOKM[:, t * P:(t + 1) * P], st6, mv)
                dve.wait_ge(rstd_ok, 2 * q + 1)
                for t in range(TPQ):
                    last = nc.vector.tensor_scalar(yn[:, t, :], TOKM[:, t * P:(t + 1) * P], mv[:, t, 0:1],
                                                   rstd[:, t:t + 1], ALU.subtract, ALU.mult)
                last.then_inc(yn_ok, 1)
                dve.wait_ge(h0_ps, q + 1)
                nc.vector.tensor_tensor(h0[:, :, :], TOKM[:, :].rearrange("p (t d) -> p t d", d=D),
                                        dbrow[:, :].unsqueeze(1).to_broadcast([P, TPQ, D]),
                                        ALU.add).then_inc(h0_ok, 1)
                dve.wait_ge(sc_ps, q + 1)
                s3 = SC[:, :].rearrange("p (a m) -> p a m", m=IMG)
                step(nc.vector.tensor_reduce(smax[:, :], s3, AX.X, ALU.max))
                settled()
                nc.vector.tensor_tensor(sc[:, :, :], s3,
                                        smax[:, :].unsqueeze(2).to_broadcast([P, TPQ * HEADS, IMG]),
                                        ALU.subtract).then_inc(sh_ok, 1)
                for j in range(4):
                    dve.wait_ge(vt_ps, 8 * q + 2 * j + 2)
                    if q and j == 0:
                        dve.wait_ge(ctx_ps, q)
                    nc.vector.tensor_copy(vblk[:, 8 * j + 4:8 * j + 8, :],
                                          VT[1][:, :].rearrange("p (i d) -> p i d", d=D)).then_inc(vt_dve, 1)
                    if j == 1:
                        dve.wait_ge(exp_ok, q + 1)
                        step(nc.vector.tensor_reduce(ssum[:, :], pe_[:, :, :], AX.X, ALU.add))
                        settled()
                        step(nc.vector.reciprocal(srec[:, :], ssum[:, :]))
                        settled()
                        nc.vector.tensor_tensor(pn[:, :, :], pe_[:, :, :],
                                                srec[:, :].unsqueeze(2).to_broadcast([P, TPQ * HEADS, IMG]),
                                                ALU.mult).then_inc(pn_ok, 1)
                dve.wait_ge(att_ps, q + 1)
                step(nc.vector.tensor_tensor(res[:, :, :], ATT[:, :].rearrange("p (t d) -> p t d", d=D),
                                             h0[:, :, :], ALU.add))
                settled()
                stats(lambda t: res[:, t, :], st6b, mvb)
                dve.wait_ge(rstd_ok, 2 * q + 2)
                for t in range(TPQ):
                    last = nc.vector.tensor_scalar(x1[:, q * TPQ + t, :], res[:, t, :], mvb[:, t, 0:1],
                                                   rstdb[:, t:t + 1], ALU.subtract, ALU.mult)
                last.then_inc(x1_ok, 1)
                dve.wait_ge(lg_ps, q + 1)
                lv = LG[:, 0:TPQ * GR * 4].rearrange("p (t c) -> p t c", c=GR * 4)
                step(nc.vector.tensor_tensor(lg[:, :, :].rearrange("p (t g) e -> p t (g e)", g=GR), lv,
                                             br[:, :].unsqueeze(1).to_broadcast([P, TPQ, GR * 4]), ALU.add))
                settled()
                step(nc.vector.tensor_reduce(lmax[:, :], lg[:, :, :], AX.X, ALU.max))
                settled()
                b4 = lambda a: a[:, :].unsqueeze(2).to_broadcast([P, R, 4])
                nc.vector.tensor_tensor(lsh[:, :, :], lg[:, :, :], b4(lmax), ALU.subtract).then_inc(lsh_ok, 1)
                dve.wait_ge(lex_ok, q + 1)
                step(nc.vector.tensor_reduce(lsum[:, :], lex[:, :, :], AX.X, ALU.add))
                settled()
                step(nc.vector.reciprocal(lrec[:, :], lsum[:, :]))
                settled()
                step(nc.vector.tensor_tensor(gp[:, :, :], lex[:, :, :], b4(lrec), ALU.mult))
                settled()
                other = gp[:, :, :].unsqueeze(2).to_broadcast([P, R, 4, 4])
                own = gp[:, :, :].unsqueeze(3).to_broadcast([P, R, 4, 4])
                trilb = tril[:, :, :].rearrange("p i j -> p (i j)").unsqueeze(1).to_broadcast([P, R, 16])
                f2 = lambda a: a[:, :, :, :].rearrange("p r i j -> p r (i j)")
                step(nc.vector.tensor_tensor(gt[:, :, :, :], other, own, ALU.is_gt))
                step(nc.vector.tensor_tensor(eq[:, :, :, :], other, own, ALU.is_equal))
                step(nc.vector.tensor_reduce(p1[:, :], gp[:, :, :], AX.X, ALU.max))
                settled()
                step(nc.vector.tensor_tensor(f2(eqt), f2(eq), trilb, ALU.mult))
                settled()
                step(nc.vector.tensor_tensor(f2(gte), f2(gt), f2(eqt), ALU.add))
                settled()
                step(nc.vector.tensor_reduce(rank[:, :, :], gte[:, :, :, :], AX.X, ALU.add))
                settled()
                step(nc.vector.tensor_scalar(first[:, :, :], rank[:, :, :], 0.0, None, ALU.is_equal))
                step(nc.vector.tensor_scalar(second[:, :, :], rank[:, :, :], 1.0, None, ALU.is_equal))
                settled()
                step(nc.vector.tensor_tensor(psec[:, :, :], gp[:, :, :], second[:, :, :], ALU.mult))
                settled()
                step(nc.vector.tensor_reduce(p2[:, :], psec[:, :, :], AX.X, ALU.add))
                settled()
                step(nc.vector.tensor_tensor(cum[:, :], p1[:, :], p2[:, :], ALU.add))
                settled()
                step(nc.vector.tensor_scalar(keep2[:, :], cum[:, :], 0.9, None, ALU.is_le))
                settled()
                step(nc.vector.tensor_tensor(kept[:, :, :], second[:, :, :], b4(keep2), ALU.mult))
                settled()
                step(nc.vector.tensor_tensor(mask[:, :, :], first[:, :, :], kept[:, :, :], ALU.add))
                settled()
                step(nc.vector.tensor_tensor(mp[:, :, :], gp[:, :, :], mask[:, :, :], ALU.mult))
                settled()
                step(nc.vector.tensor_reduce(msum[:, :], mp[:, :, :], AX.X, ALU.add))
                settled()
                step(nc.vector.tensor_scalar(msum[:, :], msum[:, :], 1e-9, None, ALU.add))
                settled()
                step(nc.vector.reciprocal(mrec[:, :], msum[:, :]))
                settled()
                step(nc.vector.tensor_tensor(wn[:, :, :], mp[:, :, :], b4(mrec), ALU.mult))
                settled()
                wv = wn[:, :, :].rearrange("p (t g) e -> p t g e", g=GR)
                for t in range(TPQ):
                    step(nc.vector.scalar_tensor_tensor(
                        out=tw[:, q * TPQ + t, :, :], in0=wv[:, t, 0, :].unsqueeze(2).to_broadcast([P, G, EPG]),
                        scalar=float(G ** -0.5), in1=wv[:, t, 1:GR, :], op0=ALU.mult, op1=ALU.mult))
            step(nc.vector.tensor_copy(acc[:, :, :], x1[:, :, :]))
            settled()

            def gated(n, s):
                dve.wait_ge(act_ok, n + 1)
                nc.vector.tensor_tensor(gu[:, s, :, :].rearrange("p c t -> p (c t)"), act[:, s, :],
                                        bank[2 * s + 1][:, :], ALU.mult).then_inc(gu_ok, 1)

            with dve.Fori(0, E) as e:
                for t in range(TILES):
                    n = e * TILES + t
                    gated(n, t % 2)
                    dve.wait_ge(y_ps, n + 1)
                    dve.wait_ge(acc_ok, n)
                    nc.vector.scalar_tensor_tensor(
                        out=acc[:, t, :], in0=bank[6 + t % 2][:, 0:D],
                        scalar=tw[:, t, :, :].rearrange("p g e -> p (g e)")[:, bass.ds(e, 1)],
                        in1=acc[:, t, :], op0=ALU.mult, op1=ALU.add).then_inc(acc_ok, 1)
            dve.wait_ge(acc_ok, NSTEPS)
            for qq in range(NQ):
                stats(lambda t: acc[:, qq * TPQ + t, :], st6b, mvb)
                dve.wait_ge(rstd_ok, 2 * NQ + qq + 1)
                for t in range(TPQ):
                    i = qq * TPQ + t
                    nc.vector.tensor_scalar(acc[:, i, :], acc[:, i, :], mvb[:, t, 0:1],
                                            rstdb[:, t:t + 1], ALU.subtract, ALU.mult).then_inc(fin_ok, 1)
                dve.wait_ge(fin_ok, (qq + 1) * TPQ)

        @block.tensor
        def _(pe):
            T = nc.tensor
            pe.wait_ge(wconv_ok, 1)
            pe.wait_ge(ident_ok, 1)
            pe.wait_ge(dma_c, 160)

            def conv(q):
                s = q % 2
                pe.wait_ge(x_in[s], 32 * (q // 2 + 1))
                if q:
                    pe.wait_ge(yct_ok, q)
                for ch in range(CH):
                    k = P if ch < 6 else RIM
                    last = T.matmul(CONV[:, :], wconv[0:k, ch, :], xcol[0:k, s, ch, :],
                                    start=(ch == 0), stop=(ch == CH - 1))
                last.then_inc(conv_ok, 1)

            def transposes(dst, src):
                for t in range(TPQ):
                    last = T.transpose(dst[:, t * P:(t + 1) * P], src(t), ident[:, :])
                return last

            tile = lambda a: (lambda t: a[:, t * P:(t + 1) * P])
            heads3 = lambda a: (lambda t: a[:, t * HEADS:(t + 1) * HEADS, :].rearrange("p h m -> p (h m)"))
            of_image = lambda a, i: a[:, :, :].rearrange("p h t -> p (h t)")[:, i:HEADS * QT:IPQ]
            conv(0)
            for q in range(NQ):
                pe.wait_ge(yct_ok, q + 1)
                if q:
                    pe.wait_ge(x1_ok, q)
                transposes(TOKM, tile(ycT)).then_inc(ytok_ok, 1)
                pe.wait_ge(yn_ok, q + 1)
                if q:
                    pe.wait_ge(vt_act, 4 * q)
                    pe.wait_ge(vt_dve, 4 * q)
                transposes(NORM, lambda t: yn[:, t, :]).then_inc(ynt_ok, 1)
                pe.wait_ge(yt_ok, q + 1)
                T.matmul(H0T[:, :], dw[:, :], yT[:, :], start=True, stop=True).then_inc(h0t_ps, 1)
                for t in range(TPQ):
                    last = T.matmul(TOKM[:, t * P:(t + 1) * P], yT[:, t * P:(t + 1) * P], dw[:, :],
                                    start=True, stop=True)
                last.then_inc(h0_ps, 1)
                pe.wait_ge(h0t_ok, q + 1)
                if q:
                    pe.wait_ge(x1t_ok, q)
                    pe.wait_ge(lsh_ok, q)
                for i, (dst, done) in enumerate(((KB, k_ps), (VB, v_ps), (QB, q_ps))):
                    j = (1, 2, 0)[i]
                    T.matmul(dst[:, :], wqkv[:, j * D:(j + 1) * D], h0T[:, :], start=True,
                             stop=True).then_inc(done, 1)
                if q + 1 < NQ:
                    conv(q + 1)
                pe.wait_ge(kblk_in, 128 * (q + 1))
                pe.wait_ge(q_ok, q + 1)
                if q:
                    pe.wait_ge(st_ok, q)
                for i in range(IPQ):
                    last = T.matmul(ST[:, i * IMG:(i + 1) * IMG], of_image(kblk, i),
                                    qT[:, i:QT:IPQ], start=True, stop=True)
                last.then_inc(st_ps, 1)

                def value_fill(f):
                    if f >= 2:
                        pe.wait_ge((vt_act, vt_dve)[f % 2], 4 * q + f // 2)
                    for i in range(4 * f, 4 * f + 4):
                        last = T.transpose(VT[f % 2][:, (i % 4) * D:(i % 4 + 1) * D],
                                           of_image(vblkT, i), ident[:, :])
                    last.then_inc(vt_ps, 1)

                pe.wait_ge(vblk_in, 128 * (q + 1))
                value_fill(0)
                value_fill(1)
                pe.wait_ge(st_ok, q + 1)
                transposes(SC, tile(sT)).then_inc(sc_ps, 1)
                for f in range(2, 8):
                    value_fill(f)
                pe.wait_ge(pn_ok, q + 1)
                pe.wait_ge(k_ok, q + 1)
                transposes(PT, heads3(pn)).then_inc(pt_ps, 1)
                pe.wait_ge(pt_ok, q + 1)
                pe.wait_ge(v_ok, q + 1)
                pe.wait_ge(vt_act, 4 * q + 4)
                pe.wait_ge(vt_dve, 4 * q + 4)
                for i in range(IPQ):
                    last = T.matmul(CTX[:, i * IMG:(i + 1) * IMG], vblk[:, i, :],
                                    pT[:, i * IMG:(i + 1) * IMG], start=True, stop=True)
                last.then_inc(ctx_ps, 1)
                pe.wait_ge(ctx_ok, q + 1)
                pe.wait_ge(h0_ok, q + 1)
                for t in range(TPQ):
                    last = T.matmul(ATT[:, t * P:(t + 1) * P], ctxT[:, t * P:(t + 1) * P], wo[:, :],
                                    start=True, stop=True)
                last.then_inc(att_ps, 1)
                pe.wait_ge(x1_ok, q + 1)
                transposes(X1T, lambda t: x1[:, q * TPQ + t, :]).then_inc(x1t_ps, 1)
                pe.wait_ge(x1t_ok, q + 1)
                for t in range(TPQ):
                    i = q * TPQ + t
                    last = T.matmul(LG[:, t * GR * 4:(t + 1) * GR * 4], x1T[:, i * P:(i + 1) * P], wr[:, :],
                                    start=True, stop=True)
                last.then_inc(lg_ps, 1)

            pe.wait_ge(lsh_ok, NQ)

            with pe.Fori(0, E // 2) as e2:
                for half in range(2):
                    pe.wait_ge(w_in[half], e2 * 48 + 48)
                    for t in range(TILES):
                        n = e2 * (2 * TILES) + half * TILES + t
                        s = t % 2
                        up, gate = bank[2 * s], bank[2 * s + 1]
                        lhs = x1T[:, t * P:(t + 1) * P]
                        if not (half == 0 and t < 2):
                            pe.wait_ge(gu_ok, n - 1)
                        else:
                            pe.wait_ge(gu_ok, e2 * (2 * TILES) if t == 0 else e2 * (2 * TILES))
                        T.matmul(up[:, :], lhs, w1s[:, half, :], start=True, stop=True)
                        T.matmul(gate[:, :], lhs, w3s[:, half, :], start=True, stop=True).then_inc(up_ps, 1)
                        pe.wait_ge(gu_ok, n + 1)
                        for c4 in range(HC):
                            last = T.transpose(bank[4 + s][:, c4 * P:(c4 + 1) * P], gu[:, s, c4, :], ident[:, :])
                        last.then_inc(gut_ps, 1)
                        pe.wait_ge(gut_ok, n + 1)
                        if half or t >= 2:
                            pe.wait_ge(acc_ok, n - 1)
                        else:
                            pe.wait_ge(acc_ok, e2 * (2 * TILES))
                        for c4 in range(HC):
                            last = T.matmul(bank[6 + s][:, 0:D], guT[:, s, c4, :], w2s[:, half, c4, :],
                                            start=(c4 == 0), stop=(c4 == HC - 1))
                        last.then_inc(y_ps, 1)


def host_layout(x, conv_w):
    import numpy as np
    x = np.asarray(x)
    w = np.asarray(conv_w)
    B = x.shape[0]
    S = 16
    xp = np.zeros((B, 66, 66, 3), x.dtype)
    xp[:, 1:65, 1:65] = x
    main = x.reshape(NQ, IPQ, 4, S, 4, S, 3).transpose(3, 5, 6, 0, 2, 4, 1).reshape(6, P, NQ, QT)
    main = np.ascontiguousarray(main.transpose(2, 1, 0, 3))
    cols = np.stack([xp[:, 1:65, 0:64:S], xp[:, 1:65, 17:66:S]])
    cols = cols.reshape(2, NQ, IPQ, 4, S, 4, 3).transpose(0, 4, 6, 1, 3, 5, 2).reshape(RIM, NQ, QT)
    rows = np.stack([xp[:, 0:64:S, 1:65], xp[:, 17:66:S, 1:65]])
    rows = rows.reshape(2, NQ, IPQ, 4, 4, S, 3).transpose(0, 5, 6, 1, 3, 4, 2).reshape(RIM, NQ, QT)
    rim = np.ascontiguousarray(np.stack([cols, rows]).transpose(2, 1, 0, 3))
    c, r, l, d, u = (w[:, :, 3 * i:3 * i + 3] for i in range(5))
    t = np.zeros((5, S, S, 3, D), w.dtype)
    t[0] = c
    t[1][:, :-1] = r[:, 1:]
    t[2][:, 1:] = l[:, :-1]
    t[3][:-1] = d[1:]
    t[4][1:] = u[:-1]
    taps = np.ascontiguousarray(t.reshape(5, 6, P, D).transpose(2, 0, 1, 3))
    wrim = np.stack([np.stack([r[:, 0], l[:, S - 1]]).reshape(RIM, D),
                     np.stack([d[0], u[S - 1]]).reshape(RIM, D)])
    return main, rim, taps, np.ascontiguousarray(wrim.transpose(1, 0, 2))


def kernel(**inputs):
    import numpy as np
    import concourse.bacc as bacc
    from concourse.bass_utils import run_bass_kernel_spmd

    g = {k: np.asarray(v) for k, v in inputs.items()}
    main, rim, taps, wrim = host_layout(g["x"], g["L0_tok_conv_w"])
    wroute = np.concatenate([g["L0_ffn_Wr"], g["L0_ffn_Wgate"].transpose(1, 0, 2).reshape(D, 16)], axis=1)
    broute = np.concatenate([g["L0_ffn_br"], g["L0_ffn_bgate"].reshape(16)])
    arrays = {
        "xmain": main, "xrim": rim, "taps": taps, "wrim": wrim,
        "conv_b": g["L0_tok_conv_b"], "gamma": g["L0_tok_gamma"], "beta": g["L0_tok_beta"],
        "dense_w": g["L0_tok_dense_w"], "dense_b": g["L0_tok_dense_b"],
        "wqkv_t": g["L0_attn_w_qkv"].T, "wo_t": g["L0_attn_w_o"].T,
        "wroute": wroute, "broute": broute,
        "w1": g["L0_ffn_W1"], "w3": g["L0_ffn_W3"],
        "w2": g["L0_ffn_W2"].reshape(E, HC, P, D).transpose(0, 2, 1, 3),
    }
    arrays = {k: np.ascontiguousarray(v) for k, v in arrays.items()}
    nc = bacc.Bacc("TRN2", target_bir_lowering=False, num_devices=1)
    args = [nc.dram_tensor(f"in_{k}", v.shape, mybir.dt.from_np(v.dtype), kind="ExternalInput").ap()
            for k, v in arrays.items()]
    out = nc.dram_tensor("out", (P, TILES, D), F32, kind="ExternalOutput").ap()
    build_program(nc, *args, out)
    r = run_bass_kernel_spmd(nc, [{f"in_{k}": v for k, v in arrays.items()}], core_ids=[0])
    got = r.results[0]["out"]
    got = got.transpose(1, 0, 2).reshape(NQ, IMG, IPQ, D).transpose(0, 2, 1, 3)
    return np.ascontiguousarray(got).reshape(NQ * IPQ, IMG, D)
```

```python
from contextlib import ExitStack

import concourse.bass as bass
from concourse import mybir

ALU = mybir.AluOpType
ACT = mybir.ActivationFunctionType
AX = mybir.AxisListType
F32 = mybir.dt.float32
I32 = mybir.dt.int32
U32 = mybir.dt.uint32

P = 128
D = 128
TOKENS = 2048
QT = 512
NQ = TOKENS // QT
TPQ = QT // P
IMG = 16
IPQ = QT // IMG
HEADS = 8
DK = D // HEADS
SCALE = DK ** -0.5
G = 4
EPG = 4
E = G * EPG
GR = G + 1
HID = 512
HC = HID // P
TILES = TOKENS // P
CH = 8
RIM = 96
CAP = TOKENS + P
DUMMY = E * CAP
ROWS = DUMMY + 4 * P
META = E + 1
ROW = D + META
WEXP = 2 * HID + HC * D
MAXT = P
K = 4
SKIP = 4 * ROWS
TOK_EPS = 1e-3
LN_EPS = 1e-5


def build_program(nc, xmain, xrim, taps, wrim, conv_b, gamma, beta, dense_w, dense_b, wqkv_t,
                  wo_t, wroute, broute, wexp,
                  lists, sums_even, sums_odd, out):
    sums = [sums_even, sums_odd]
    ctx = ExitStack()
    with ctx:
        def sb(name, shape, dt=F32):
            return ctx.enter_context(nc.sbuf_tensor(name, shape, dt))

        def sem(name):
            return ctx.enter_context(nc.semaphore(name))

        bank = [ctx.enter_context(nc.psum_tensor(f"bank{i}", [P, 512], F32)) for i in range(8)]
        CONV, TOKM, NORM, H0T, QB, KB, VB, ST = bank
        VT = [NORM, H0T]
        SC, PT, CTX, ATT = QB, KB, VB, TOKM
        X1T, LG = QB, KB

        ident = sb("ident", [P, P])
        wall = sb("wall", [P, E * WEXP])
        half = E // 2 * WEXP
        xcol = wall[:, half:half + 2 * CH * QT].rearrange("p (s c t) -> p s c t", s=2, c=CH)
        tapsum = wall[:, half + 2 * CH * QT:half + 2 * CH * QT + 30 * D].rearrange(
            "p (a c d) -> p a c d", a=5, c=6)
        wconv = sb("wconv", [P, CH, D])
        convb = sb("convb", [P, 1])
        gam = sb("gam", [P, 1])
        bet = sb("bet", [P, 1])
        dw = sb("dw", [P, D])
        dbcol = sb("dbcol", [P, 1])
        dbrow = sb("dbrow", [P, D])
        wqkv = sb("wqkv", [P, 3 * D])
        wo = sb("wo", [P, D])
        wr = sb("wr", [P, GR * 4])
        br = sb("br", [P, GR * 4])
        mhalf = sb("mhalf", [P, TPQ])
        tril = sb("tril", [P, 4, 4])
        ycT = sb("ycT", [P, QT])
        st6 = sb("st6", [P, TPQ, 6])
        mv = sb("mv", [P, TPQ, 2])
        rstd = sb("rstd", [P, TPQ])
        st6b = sb("st6b", [P, TPQ, 6])
        mvb = sb("mvb", [P, TPQ, 2])
        rstdb = sb("rstdb", [P, TPQ])
        veps = sb("veps", [P, TPQ])
        vepsb = sb("vepsb", [P, TPQ])
        yn = sb("yn", [P, TPQ, D])
        yT = sb("yT", [P, QT])
        h0 = sb("h0", [P, TPQ, D])
        h0T = sb("h0T", [P, QT])
        qT = sb("qT", [P, QT])
        kT = sb("kT", [P, QT])
        vT = sb("vT", [P, QT])
        kblk = sb("kblk", [P, HEADS, QT])
        vblkT = sb("vblkT", [P, HEADS, QT])
        vblk = sb("vblk", [P, IPQ, D])
        sT = sb("sT", [P, QT])
        sc = sb("sc", [P, TPQ * HEADS, IMG])
        smax = sb("smax", [P, TPQ * HEADS])
        ssum = sb("ssum", [P, TPQ * HEADS])
        srec = sb("srec", [P, TPQ * HEADS])
        pT = sb("pT", [P, QT])
        ctxT = sb("ctxT", [P, QT])
        res = sb("res", [P, TPQ, D])
        rows = sb("rows", [P, TILES, ROW])
        x1 = rows[:, :, 0:D]
        x1T = sb("x1T", [P, QT])
        R = TPQ * GR
        lg = sb("lg", [P, R, 4])
        lmax = sb("lmax", [P, R])
        lsh = sb("lsh", [P, R, 4])
        lex = sb("lex", [P, R, 4])
        lsum = sb("lsum", [P, R])
        lrec = sb("lrec", [P, R])
        gp = sb("gp", [P, R, 4])
        gt = sb("gt", [P, R, 4, 4])
        eq = sb("eq", [P, R, 4, 4])
        rank = sb("rank", [P, R, 4])
        first = sb("first", [P, R, 4])
        second = sb("second", [P, R, 4])
        psec = sb("psec", [P, R, 4])
        p1 = sb("p1", [P, R])
        p2 = sb("p2", [P, R])
        cum = sb("cum", [P, R])
        keep2 = sb("keep2", [P, R])
        kept = sb("kept", [P, R, 4])
        mask = sb("mask", [P, R, 4])
        mp = sb("mp", [P, R, 4])
        msum = sb("msum", [P, R])
        mrec = sb("mrec", [P, R])
        wn = sb("wn", [P, R, 4])
        sel = sb("sel", [P, TPQ, E])
        before = sb("before", [P, P])
        ones = sb("ones", [P, P])
        base = sb("base", [P, TPQ + 1, E])
        pos = sb("pos", [P, TPQ, E])
        pick = sb("pick", [P, K, TPQ, E])
        picked = sb("picked", [P, K, TPQ, E])
        taken = sb("taken", [P, K, TPQ])
        place = sb("place", [P, K, TPQ])
        idx = sb("idx", [P, NQ, K * TPQ], I32)
        tile_no = sb("tile_no", [P, 1])
        firsts = sb("firsts", [P, E])
        steps16 = sb("steps16", [P, TILES + 1])
        ntl = sb("ntl", [P, E])
        ngt = sb("ngt", [P, E, TILES + 1])
        ends = sb("ends", [P, E])
        past = sb("past", [P, E])
        pastn = sb("pastn", [P, E])
        tcol = sb("tcol", [P, 4])
        tmp4 = sb("tmp4", [P, 4])
        mark = sb("mark", [1, 1])
        waited = sb("waited", [1, 2])
        expert_row = sb("expert_row", [1, MAXT], I32)
        place_row = sb("place_row", [1, MAXT], I32)
        tail_row = sb("tail_row", [1, E], I32)
        pairs = sb("pairs", [1, 1], I32)
        pairf = sb("pairf", [1, 2])
        xin = kblk[:, 0, 0:2 * P].rearrange("p (s d) -> p s d", s=2)
        xT = kblk[:, 1, 0:2 * P].rearrange("p (s d) -> p s d", s=2)
        yw = kblk[:, 2, 0:2 * D].rearrange("p (s d) -> p s d", s=2)
        filler = sb("filler", [P, ROW])
        meta = vblk[:, 0:12, :].rearrange("p a b -> p (a b)")[:, 0:84 * META]
        act = vblkT[:, 0:2, :]
        gu = vblkT[:, 2:4, :].rearrange("p s (c t) -> p s c t", t=P)
        guT = vblkT[:, 4:6, :].rearrange("p s (c t) -> p s c t", t=P)
        ids = sb("ids", [P, 2], I32)
        acc = wall[:, 0:2 * TILES * D].rearrange("p (a t d) -> p a t d", a=2, t=TILES)

        dma_w = sem("dma_w")
        dma_c = sem("dma_c")
        x_in = [sem("x_in0"), sem("x_in1")]
        zeros = sem("zeros")
        ident_ok = sem("ident_ok")
        pool_c = sem("pool_c")
        wconv_ok = sem("wconv_ok")
        conv_ok = sem("conv_ok")
        yct_ok = sem("yct_ok")
        ytok_ok = sem("ytok_ok")
        var_ok = sem("var_ok")
        rstd_ok = sem("rstd_ok")
        yn_ok = sem("yn_ok")
        ynt_ok = sem("ynt_ok")
        yt_ok = sem("yt_ok")
        h0_ps = sem("h0_ps")
        h0t_ps = sem("h0t_ps")
        h0_ok = sem("h0_ok")
        h0t_ok = sem("h0t_ok")
        q_ps = sem("q_ps")
        k_ps = sem("k_ps")
        v_ps = sem("v_ps")
        q_ok = sem("q_ok")
        k_ok = sem("k_ok")
        v_ok = sem("v_ok")
        kblk_in = sem("kblk_in")
        vblk_in = sem("vblk_in")
        vt_ps = sem("vt_ps")
        vt_act = sem("vt_act")
        vt_dve = sem("vt_dve")
        st_ps = sem("st_ps")
        st_ok = sem("st_ok")
        sc_ps = sem("sc_ps")
        sh_ok = sem("sh_ok")
        exp_ok = sem("exp_ok")
        pn_ok = sem("pn_ok")
        pt_ps = sem("pt_ps")
        pt_ok = sem("pt_ok")
        ctx_ps = sem("ctx_ps")
        ctx_ok = sem("ctx_ok")
        att_ps = sem("att_ps")
        x1_ok = sem("x1_ok")
        x1t_ps = sem("x1t_ps")
        x1t_ok = sem("x1t_ok")
        lg_ps = sem("lg_ps")
        lsh_ok = sem("lsh_ok")
        lex_ok = sem("lex_ok")
        pool_s = sem("pool_s")
        dve_s = sem("dve_s")
        w_in = sem("w_in")
        init_done = sem("init_done")
        filler_ok = sem("filler_ok")
        sel_ok = sem("sel_ok")
        count_ps = sem("count_ps")
        idx_ok = sem("idx_ok")
        scattered = sem("scattered")
        tcol_ok = sem("tcol_ok")
        trow_ps = sem("trow_ps")
        table_ok = sem("table_ok")
        tails = sem("tails")
        xtile_in = [sem("xtile_in0"), sem("xtile_in1")]
        xt_ps = sem("xt_ps")
        xt_ok = sem("xt_ok")
        yw_ok = sem("yw_ok")
        added = [sem("added0"), sem("added1")]
        sums_in = sem("sums_in")
        up_ps = sem("up_ps")
        act_ok = sem("act_ok")
        gu_ok = sem("gu_ok")
        gut_ps = sem("gut_ps")
        gut_ok = sem("gut_ok")
        y_ps = sem("y_ps")
        ids_ok = sem("ids_ok")
        carried = sem("carried")
        fin_ok = sem("fin_ok")
        out_done = sem("out_done")

        block = ctx.enter_context(nc.Block())

        @block.sync
        def _(sp):
            sp.dma_start(tapsum[:, :, :, :], taps).then_inc(dma_w, 16)
            sp.dma_start(wconv[0:RIM, 6:8, :], wrim).then_inc(dma_w, 16)

            def load_x(q, slot):
                sp.dma_start(xcol[:, slot, 0:6, :], xmain[q]).then_inc(x_in[slot], 16)
                sp.dma_start(xcol[0:RIM, slot, 6:8, :], xrim[q]).then_inc(x_in[slot], 16)

            load_x(0, 0)
            load_x(1, 1)

            def blocks(q):
                sp.wait_ge(zeros, 2)
                sp.wait_ge(k_ok, q + 1)
                sp.wait_ge(st_ps, q)
                for h in range(HEADS):
                    sp.dma_start(kblk[DK * h:DK * (h + 1), h, :],
                                 kT[DK * h:DK * (h + 1), :]).then_inc(kblk_in, 16)
                sp.wait_ge(v_ok, q + 1)
                sp.wait_ge(vt_ps, 8 * q)
                for h in range(HEADS):
                    sp.dma_start(vblkT[DK * h:DK * (h + 1), h, :],
                                 vT[DK * h:DK * (h + 1), :]).then_inc(vblk_in, 16)

            for q in range(NQ):
                if q + 2 < NQ:
                    sp.wait_ge(conv_ok, q + 1)
                    load_x(q + 2, q % 2)
                blocks(q)

            sp.wait_ge(conv_ok, NQ)
            for e in range(E // 2, E):
                sp.dma_start(wall[:, e * WEXP:(e + 1) * WEXP], wexp[e]).then_inc(w_in, 16)

            sp.wait_ge(table_ok, 1)
            with sp.Fori(0, E) as e:
                at = sp.value_load(tail_row[0:1, bass.ds(e, 1)], min_val=0, max_val=DUMMY - P)
                sp.dma_start(lists[bass.ds(at, P), :], filler[:, :]).then_inc(tails, 16)
            sp.wait_ge(tails, 16 * E)
            sp.wait_ge(scattered, 16 * K * TILES)

            def load_tile(i, s):
                at = sp.value_load(place_row[0:1, bass.ds(i, 1)], min_val=0, max_val=ROWS - P)
                sp.dma_start(xin[:, s, :], lists[bass.ds(at, P), 0:D]).then_inc(xtile_in[s], 16)
                sp.dma_start(meta[:, bass.ds(i * META, META)], lists[bass.ds(at, P), D:ROW]).then_inc(xtile_in[s], 16)

            load_tile(0, 0)
            load_tile(1, 1)
            npairs = sp.value_load(pairs[0:1, 0:1], min_val=1, max_val=40)
            with sp.Fori(0, npairs) as j:
                for s in range(2):
                    sp.wait_ge(xt_ps, j * 2 + (s + 1))
                    load_tile(j * 2 + (s + 2), s)
            sp.wait_ge(xt_ps, npairs * 2 + 1)
            load_tile(npairs * 2 + 2, 0)
            for a in range(2):
                sp.wait_ge(added[a], npairs * 16 + 16)
                sp.dma_start(acc[:, a, :, :], sums[a][0:TOKENS, :].rearrange("(p t) d -> p t d", t=TILES)
                             ).then_inc(sums_in, 16)
            sp.wait_ge(fin_ok, TILES)
            sp.dma_start(out, acc[:, 0, :, :]).then_inc(out_done, 16)
            sp.wait_ge(out_done, 16)

        @block.gpsimd
        def _(pool):
            pool.memset(ident[:, :], 0.0).then_inc(pool_c, 1)
            pool.wait_ge(pool_c, 1)
            pool.affine_select(out=ident[:, :], in_=ident[:, :], compare_op=ALU.not_equal, fill=1.0,
                               base=0, pattern=[[-1, P]], channel_multiplier=1).then_inc(ident_ok, 1)
            pool.memset(filler[:, :], 0.0).then_inc(filler_ok, 1)
            pool.wait_ge(filler_ok, 1)
            pool.iota(filler[:, ROW - 1:ROW].bitcast(I32), pattern=[[0, 1]], base=TOKENS,
                      channel_multiplier=1).then_inc(filler_ok, 1)
            pool.iota(rows[:, :, ROW - 1:ROW].bitcast(I32), pattern=[[1, TILES], [0, 1]], base=0,
                      channel_multiplier=TILES).then_inc(ident_ok, 1)
            pool.memset(mhalf[:, :], -0.5).then_inc(pool_c, 1)
            pool.memset(tril[:, :, :], 1.0).then_inc(pool_c, 1)
            pool.wait_ge(pool_c, 3)
            pool.affine_select(out=tril[:, :, :], in_=tril[:, :, :], compare_op=ALU.is_gt, fill=0.0,
                               base=0, pattern=[[1, 4], [-1, 4]], channel_multiplier=0).then_inc(ident_ok, 1)
            pool.memset(ones[:, :], 1.0).then_inc(ident_ok, 1)
            pool.memset(before[:, :], 1.0).then_inc(pool_c, 1)
            pool.wait_ge(pool_c, 4)
            pool.affine_select(out=before[:, :], in_=before[:, :], compare_op=ALU.is_gt, fill=0.0,
                               base=0, pattern=[[1, P]], channel_multiplier=-1).then_inc(ident_ok, 1)
            for dst, pat, mul in ((tile_no[:, :], [[0, 1]], 1), (firsts[:, :], [[CAP, E]], 0),
                                  (steps16[:, :], [[P, TILES + 1]], 0)):
                pool.iota(dst, pattern=pat, base=0, channel_multiplier=mul,
                          allow_small_or_imprecise_dtypes=True).then_inc(ident_ok, 1)
            pool.memset(kblk[:, :, :], 0.0).then_inc(zeros, 1)
            pool.memset(vblkT[:, :, :], 0.0).then_inc(zeros, 1)
            steps = [0]

            def rsqrt(dst, tmp, var, eps):
                pool.tensor_scalar(tmp, var, eps, None, ALU.add).then_inc(pool_s, 1)
                steps[0] += 1
                pool.wait_ge(pool_s, steps[0])
                pool.tensor_tensor(dst, tmp, mhalf[:, :], ALU.pow).then_inc(rstd_ok, 1)

            for q in range(NQ):
                pool.wait_ge(var_ok, 2 * q + 1)
                rsqrt(rstd[:, :], veps[:, :], mv[:, :, 1], TOK_EPS)
                pool.wait_ge(var_ok, 2 * q + 2)
                rsqrt(rstdb[:, :], vepsb[:, :], mvb[:, :, 1], LN_EPS)
                pool.wait_ge(idx_ok, q + 1)
                for k in range(K):
                    for t in range(TPQ):
                        pool.indirect_dma_start(
                            out=lists, out_offset=bass.IndirectOffsetOnAxis(
                                ap=idx[:, q, k * TPQ + t:k * TPQ + t + 1].bitcast(U32), axis=0),
                            in_=rows[:, q * TPQ + t, :], in_offset=None,
                            bounds_check=ROWS - 1, oob_is_err=False).then_inc(scattered, 16)
            pool.memset(mark[:, :], 0.0).then_inc(carried, 1)
            pool.wait_ge(init_done, 48)
            for s in range(2):
                pool.indirect_dma_start(
                    out=sums[s], out_offset=bass.IndirectOffsetOnAxis(
                        ap=filler[:, ROW - 1:ROW].bitcast(U32), axis=0),
                    in_=filler[:, 0:D], in_offset=None, bounds_check=TOKENS + P - 1,
                    compute_op=ALU.add).then_inc(added[s], 16)
            pool.wait_ge(table_ok, 1)
            npairs = pool.value_load(pairs[0:1, 0:1], min_val=1, max_val=40)
            with pool.Fori(0, npairs) as j:
                for s in range(2):
                    pool.wait_ge(yw_ok, j * 2 + (s + 2))
                    pool.wait_ge(added[s], j * 16 + 16)
                    pool.wait_ge(carried, j * 2 + (s + 1))
                    pool.tensor_tensor(waited[:, s:s + 1], mark[:, :], mark[:, :], ALU.add).then_inc(carried, 1)
                    pool.indirect_dma_start(
                        out=sums[s], out_offset=bass.IndirectOffsetOnAxis(ap=ids[:, s:s + 1].bitcast(U32), axis=0),
                        in_=yw[:, s, :], in_offset=None, bounds_check=TOKENS + P - 1,
                        compute_op=ALU.add).then_inc(added[s], 16)
            for t in range(NQ):
                pool.wait_ge(var_ok, 2 * NQ + t + 1)
                rsqrt(rstdb[:, :], vepsb[:, :], mvb[:, :, 1], LN_EPS)

        @block.scalar
        def _(ac):
            for dst, src in ((convb[:, :], conv_b), (gam[:, :], gamma), (bet[:, :], beta),
                             (dbcol[:, :], dense_b)):
                ac.dma_start(dst, src.rearrange("(p a) -> p a", a=1)).then_inc(dma_c, 16)
            for dst, src in ((dw, dense_w), (wqkv, wqkv_t), (wo, wo_t), (wr, wroute)):
                ac.dma_start(dst[:, :], src).then_inc(dma_c, 16)
            ac.dma_start(dbrow[:, :], dense_b.partition_broadcast(P)).then_inc(dma_c, 16)
            ac.dma_start(br[:, :], broute.partition_broadcast(P)).then_inc(dma_c, 16)
            for e in range(E // 2):
                ac.dma_start(wall[:, e * WEXP:(e + 1) * WEXP], wexp[e]).then_inc(w_in, 16)
            ac.wait_ge(filler_ok, 2)
            for a in range(2):
                ac.dma_start(sums[a].rearrange("(n p) d -> p n d", p=P),
                             filler[:, 0:D].unsqueeze(1).to_broadcast([P, TILES + 1, D])).then_inc(init_done, 16)
            ac.dma_start(lists[DUMMY:ROWS, :].rearrange("(n p) d -> p n d", p=P),
                         filler[:, :].unsqueeze(1).to_broadcast([P, 4, ROW])).then_inc(init_done, 16)
            ac.wait_ge(dma_c, 160)

            def conv_out(q):
                ac.wait_ge(conv_ok, q + 1)
                if q:
                    ac.wait_ge(ytok_ok, q)
                ac.activation(ycT[:, :], CONV[:, :], ACT.Identity, bias=convb[:, 0:1]).then_inc(yct_ok, 1)

            conv_out(0)
            for q in range(NQ):
                ac.wait_ge(ynt_ok, q + 1)
                ac.activation(yT[:, :], NORM[:, :], ACT.Identity, bias=bet[:, 0:1],
                              scale=gam[:, 0:1]).then_inc(yt_ok, 1)
                ac.wait_ge(h0t_ps, q + 1)
                ac.activation(h0T[:, :], H0T[:, :], ACT.Identity, bias=dbcol[:, 0:1]).then_inc(h0t_ok, 1)
                ac.wait_ge(q_ps, q + 1)
                ac.activation(qT[:, :], QB[:, :], ACT.Copy, scale=SCALE).then_inc(q_ok, 1)
                ac.wait_ge(k_ps, q + 1)
                if q:
                    ac.wait_ge(kblk_in, 128 * q)
                ac.activation(kT[:, :], KB[:, :], ACT.Copy).then_inc(k_ok, 1)
                ac.wait_ge(v_ps, q + 1)
                if q:
                    ac.wait_ge(vblk_in, 128 * q)
                ac.activation(vT[:, :], VB[:, :], ACT.Copy).then_inc(v_ok, 1)
                if q + 1 < NQ:
                    conv_out(q + 1)
                ac.wait_ge(st_ps, q + 1)
                ac.activation(sT[:, :], ST[:, :], ACT.Copy).then_inc(st_ok, 1)
                for j in range(4):
                    ac.wait_ge(vt_ps, 8 * q + 2 * j + 1)
                    if q and j == 0:
                        ac.wait_ge(ctx_ps, q)
                    ac.activation(vblk[:, 8 * j:8 * j + 4, :], VT[0][:, :].rearrange("p (i d) -> p i d", d=D),
                                  ACT.Copy).then_inc(vt_act, 1)
                    if j == 1:
                        ac.wait_ge(sh_ok, q + 1)
                        ac.activation(sc[:, :, :], sc[:, :, :], ACT.Exp).then_inc(exp_ok, 1)
                ac.wait_ge(pt_ps, q + 1)
                ac.activation(pT[:, :], PT[:, :], ACT.Copy).then_inc(pt_ok, 1)
                ac.wait_ge(ctx_ps, q + 1)
                ac.activation(ctxT[:, :].rearrange("p (m i) -> p m i", i=IPQ),
                              CTX[:, :].rearrange("p (i m) -> p m i", i=IPQ), ACT.Copy).then_inc(ctx_ok, 1)
                ac.wait_ge(x1t_ps, q + 1)
                ac.activation(x1T[:, :], X1T[:, :], ACT.Copy).then_inc(x1t_ok, 1)
                ac.wait_ge(lsh_ok, q + 1)
                ac.activation(lex[:, :, :], lsh[:, :, :], ACT.Exp).then_inc(lex_ok, 1)

            def silu_of(n, s):
                ac.wait_ge(up_ps, n + 1)
                ac.activation(act[:, s, :], bank[2 * s][:, :], ACT.Silu).then_inc(act_ok, 1)

            def gut_of(n, s):
                ac.wait_ge(gut_ps, n + 1)
                ac.activation(guT[:, s, :, :], bank[4 + s][:, :].rearrange("p (c t) -> p c t", t=P),
                              ACT.Copy).then_inc(gut_ok, 1)

            ac.wait_ge(table_ok, 1)
            npairs = ac.value_load(pairs[0:1, 0:1], min_val=1, max_val=40)
            silu_of(0, 0)
            silu_of(1, 1)
            gut_of(0, 0)
            with ac.Fori(0, npairs) as j:
                for s in range(2):
                    silu_of(j * 2 + (s + 2), s)
                    gut_of(j * 2 + (s + 1), 1 - s)

        @block.vector
        def _(dve):
            N_Q = 0
            c = [0]

            def step(inst):
                inst.then_inc(dve_s, 1)
                c[0] += 1

            def settled():
                dve.wait_ge(dve_s, c[0])

            dve.wait_ge(dma_w, 32)
            tp = [tapsum[:, i, :, :] for i in range(5)]
            step(nc.vector.tensor_tensor(wconv[:, 0:6, :], tp[0], tp[1], ALU.add))
            step(nc.vector.tensor_tensor(tp[2], tp[2], tp[3], ALU.add))
            settled()
            step(nc.vector.tensor_tensor(wconv[:, 0:6, :], wconv[:, 0:6, :], tp[4], ALU.add))
            settled()
            nc.vector.tensor_tensor(wconv[:, 0:6, :], wconv[:, 0:6, :], tp[2], ALU.add).then_inc(wconv_ok, 1)
            dve.wait_ge(dma_c, 160)
            dve.wait_ge(ident_ok, 8)
            step(nc.vector.tensor_copy(base[:, 0, :], firsts[:, :]))
            settled()

            def stats(src, st, m):
                for t in range(TPQ):
                    step(nc.vector.bn_stats(st[:, t, :], src(t)))
                settled()
                for t in range(TPQ):
                    last = nc.vector.bn_aggr(m[:, t, :], st[:, t, :])
                    if t < TPQ - 1:
                        step(last)
                last.then_inc(var_ok, 1)

            for q in range(NQ):
                dve.wait_ge(ytok_ok, q + 1)
                stats(lambda t: TOKM[:, t * P:(t + 1) * P], st6, mv)
                dve.wait_ge(rstd_ok, 2 * q + 1)
                for t in range(TPQ):
                    last = nc.vector.tensor_scalar(yn[:, t, :], TOKM[:, t * P:(t + 1) * P], mv[:, t, 0:1],
                                                   rstd[:, t:t + 1], ALU.subtract, ALU.mult)
                last.then_inc(yn_ok, 1)
                dve.wait_ge(h0_ps, q + 1)
                nc.vector.tensor_tensor(h0[:, :, :], TOKM[:, :].rearrange("p (t d) -> p t d", d=D),
                                        dbrow[:, :].unsqueeze(1).to_broadcast([P, TPQ, D]),
                                        ALU.add).then_inc(h0_ok, 1)
                dve.wait_ge(sc_ps, q + 1)
                s3 = SC[:, :].rearrange("p (a m) -> p a m", m=IMG)
                step(nc.vector.tensor_reduce(smax[:, :], s3, AX.X, ALU.max))
                settled()
                nc.vector.tensor_tensor(sc[:, :, :], s3,
                                        smax[:, :].unsqueeze(2).to_broadcast([P, TPQ * HEADS, IMG]),
                                        ALU.subtract).then_inc(sh_ok, 1)
                for j in range(4):
                    dve.wait_ge(vt_ps, 8 * q + 2 * j + 2)
                    if q and j == 0:
                        dve.wait_ge(ctx_ps, q)
                    nc.vector.tensor_copy(vblk[:, 8 * j + 4:8 * j + 8, :],
                                          VT[1][:, :].rearrange("p (i d) -> p i d", d=D)).then_inc(vt_dve, 1)
                    if j == 1:
                        dve.wait_ge(exp_ok, q + 1)
                        step(nc.vector.tensor_reduce(ssum[:, :], sc[:, :, :], AX.X, ALU.add))
                        settled()
                        step(nc.vector.reciprocal(srec[:, :], ssum[:, :]))
                        settled()
                        nc.vector.tensor_tensor(sc[:, :, :], sc[:, :, :],
                                                srec[:, :].unsqueeze(2).to_broadcast([P, TPQ * HEADS, IMG]),
                                                ALU.mult).then_inc(pn_ok, 1)
                dve.wait_ge(att_ps, q + 1)
                step(nc.vector.tensor_tensor(res[:, :, :], ATT[:, :].rearrange("p (t d) -> p t d", d=D),
                                             h0[:, :, :], ALU.add))
                settled()
                stats(lambda t: res[:, t, :], st6b, mvb)
                dve.wait_ge(rstd_ok, 2 * q + 2)
                for t in range(TPQ):
                    last = nc.vector.tensor_scalar(x1[:, q * TPQ + t, :], res[:, t, :], mvb[:, t, 0:1],
                                                   rstdb[:, t:t + 1], ALU.subtract, ALU.mult)
                last.then_inc(x1_ok, 1)
                dve.wait_ge(lg_ps, q + 1)
                lv = LG[:, 0:TPQ * GR * 4].rearrange("p (t c) -> p t c", c=GR * 4)
                step(nc.vector.tensor_tensor(lg[:, :, :].rearrange("p (t g) e -> p t (g e)", g=GR), lv,
                                             br[:, :].unsqueeze(1).to_broadcast([P, TPQ, GR * 4]), ALU.add))
                settled()
                step(nc.vector.tensor_reduce(lmax[:, :], lg[:, :, :], AX.X, ALU.max))
                settled()
                b4 = lambda a: a[:, :].unsqueeze(2).to_broadcast([P, R, 4])
                nc.vector.tensor_tensor(lsh[:, :, :], lg[:, :, :], b4(lmax), ALU.subtract).then_inc(lsh_ok, 1)
                dve.wait_ge(lex_ok, q + 1)
                step(nc.vector.tensor_reduce(lsum[:, :], lex[:, :, :], AX.X, ALU.add))
                settled()
                step(nc.vector.reciprocal(lrec[:, :], lsum[:, :]))
                settled()
                step(nc.vector.tensor_tensor(gp[:, :, :], lex[:, :, :], b4(lrec), ALU.mult))
                settled()
                other = gp[:, :, :].unsqueeze(2).to_broadcast([P, R, 4, 4])
                own = gp[:, :, :].unsqueeze(3).to_broadcast([P, R, 4, 4])
                trilb = tril[:, :, :].rearrange("p i j -> p (i j)").unsqueeze(1).to_broadcast([P, R, 16])
                f2 = lambda a: a[:, :, :, :].rearrange("p r i j -> p r (i j)")
                step(nc.vector.tensor_tensor(gt[:, :, :, :], other, own, ALU.is_gt))
                step(nc.vector.tensor_tensor(eq[:, :, :, :], other, own, ALU.is_equal))
                step(nc.vector.tensor_reduce(p1[:, :], gp[:, :, :], AX.X, ALU.max))
                settled()
                step(nc.vector.tensor_tensor(f2(eq), f2(eq), trilb, ALU.mult))
                settled()
                step(nc.vector.tensor_tensor(f2(gt), f2(gt), f2(eq), ALU.add))
                settled()
                step(nc.vector.tensor_reduce(rank[:, :, :], gt[:, :, :, :], AX.X, ALU.add))
                settled()
                step(nc.vector.tensor_scalar(first[:, :, :], rank[:, :, :], 0.0, None, ALU.is_equal))
                step(nc.vector.tensor_scalar(second[:, :, :], rank[:, :, :], 1.0, None, ALU.is_equal))
                settled()
                step(nc.vector.tensor_tensor(psec[:, :, :], gp[:, :, :], second[:, :, :], ALU.mult))
                settled()
                step(nc.vector.tensor_reduce(p2[:, :], psec[:, :, :], AX.X, ALU.add))
                settled()
                step(nc.vector.tensor_tensor(cum[:, :], p1[:, :], p2[:, :], ALU.add))
                settled()
                step(nc.vector.tensor_scalar(keep2[:, :], cum[:, :], 0.9, None, ALU.is_le))
                settled()
                step(nc.vector.tensor_tensor(kept[:, :, :], second[:, :, :], b4(keep2), ALU.mult))
                settled()
                step(nc.vector.tensor_tensor(mask[:, :, :], first[:, :, :], kept[:, :, :], ALU.add))
                settled()
                step(nc.vector.tensor_tensor(mp[:, :, :], gp[:, :, :], mask[:, :, :], ALU.mult))
                settled()
                step(nc.vector.tensor_reduce(msum[:, :], mp[:, :, :], AX.X, ALU.add))
                settled()
                step(nc.vector.tensor_scalar(msum[:, :], msum[:, :], 1e-9, None, ALU.add))
                settled()
                step(nc.vector.reciprocal(mrec[:, :], msum[:, :]))
                settled()
                step(nc.vector.tensor_tensor(wn[:, :, :], mp[:, :, :], b4(mrec), ALU.mult))
                settled()
                wv = wn[:, :, :].rearrange("p (t g) e -> p t g e", g=GR)
                for t in range(TPQ):
                    step(nc.vector.scalar_tensor_tensor(
                        out=rows[:, q * TPQ + t, D:D + E].rearrange("p (g e) -> p g e", g=G),
                        in0=wv[:, t, 0, :].unsqueeze(2).to_broadcast([P, G, EPG]),
                        scalar=float(G ** -0.5), in1=wv[:, t, 1:GR, :], op0=ALU.mult, op1=ALU.mult))
                mk = mask[:, :, :].rearrange("p (t g) e -> p t g e", g=GR)
                fi = first[:, :, :].rearrange("p (t g) e -> p t g e", g=GR)
                ke = kept[:, :, :].rearrange("p (t g) e -> p t g e", g=GR)
                s4 = lambda a: a[:, :, :].rearrange("p t (g e) -> p t g e", g=G)
                over_e = lambda a: a[:, :, 0, :].unsqueeze(3).to_broadcast([P, TPQ, G, EPG])
                nc.vector.tensor_tensor(s4(sel), over_e(mk), mk[:, :, 1:GR, :], ALU.mult).then_inc(sel_ok, 1)
                for k, (a, b) in enumerate(((fi, fi), (fi, ke), (ke, fi), (ke, ke))):
                    step(nc.vector.tensor_tensor(s4(pick[:, k]), over_e(a), b[:, :, 1:GR, :], ALU.mult))
                settled()
                step(nc.vector.tensor_reduce(taken[:, :, :], pick[:, :, :, :], AX.X, ALU.add))
                dve.wait_ge(count_ps, q + 1)
                if q:
                    step(nc.vector.tensor_copy(base[:, 0, :], base[:, TPQ, :]))
                    settled()
                for t in range(TPQ):
                    step(nc.vector.tensor_tensor(base[:, t + 1, :], base[:, t, :],
                                                 LG[:, 192 + t * E:192 + (t + 1) * E], ALU.add))
                    settled()
                step(nc.vector.tensor_tensor(pos[:, :, :], LG[:, 128:192].rearrange("p (t e) -> p t e", e=E),
                                             base[:, 0:TPQ, :], ALU.add))
                settled()
                te = lambda a: a[:, :, :, :].rearrange("p k t e -> p k (t e)")
                step(nc.vector.tensor_tensor(
                    te(picked), te(pick),
                    pos[:, :, :].rearrange("p t e -> p (t e)").unsqueeze(1).to_broadcast([P, K, TPQ * E]), ALU.mult))
                step(nc.vector.tensor_scalar(taken[:, :, :], taken[:, :, :], -float(SKIP), float(SKIP),
                                             ALU.mult, ALU.add))
                settled()
                step(nc.vector.tensor_reduce(place[:, :, :], picked[:, :, :, :], AX.X, ALU.add))
                settled()
                nc.vector.tensor_tensor(idx[:, q, :].rearrange("p (k t) -> p k t", k=K), place[:, :, :],
                                        taken[:, :, :], ALU.add).then_inc(idx_ok, 1)
            rowsn = base[:, TPQ, :]
            step(nc.vector.tensor_tensor(ntl[:, :], rowsn, firsts[:, :], ALU.subtract))
            settled()
            step(nc.vector.tensor_tensor(ngt[:, :, :], ntl[:, :].unsqueeze(2).to_broadcast([P, E, TILES + 1]),
                                         steps16[:, :].unsqueeze(1).to_broadcast([P, E, TILES + 1]), ALU.is_gt))
            settled()
            step(nc.vector.tensor_reduce(ntl[:, :], ngt[:, :, :], AX.X, ALU.add))
            settled()
            step(nc.vector.tensor_tensor_scan(ends[:, :], ones[:, 0:E], ntl[:, :], 0.0, ALU.mult, ALU.add))
            settled()
            step(nc.vector.tensor_scalar(past[:, :], ends[:, :], tile_no[:, 0:1], None, ALU.is_le))
            step(nc.vector.tensor_scalar(pairf[0:1, 0:1], ends[0:1, E - 1:E], 0.5, 0.25, ALU.mult, ALU.add))
            settled()
            step(nc.vector.tensor_tensor(pastn[:, :], past[:, :], ntl[:, :], ALU.mult))
            step(nc.vector.tensor_reduce(tcol[:, 0:1], past[:, :], AX.X, ALU.add))
            settled()
            step(nc.vector.tensor_reduce(tcol[:, 1:2], pastn[:, :], AX.X, ALU.add))
            step(nc.vector.tensor_scalar(tcol[:, 2:3], tcol[:, 0:1], float(E - 1), None, ALU.min))
            step(nc.vector.tensor_scalar(tmp4[:, 0:1], tcol[:, 0:1], float(CAP), None, ALU.mult))
            settled()
            step(nc.vector.tensor_tensor(tmp4[:, 1:2], tile_no[:, :], tcol[:, 1:2], ALU.subtract))
            settled()
            nc.vector.scalar_tensor_tensor(out=tcol[:, 3:4], in0=tmp4[:, 1:2], scalar=float(P), in1=tmp4[:, 0:1],
                                           op0=ALU.mult, op1=ALU.add).then_inc(tcol_ok, 1)
            dve.wait_ge(trow_ps, 1)
            step(nc.vector.tensor_copy(expert_row[:, :], LG[0:1, 0:P]))
            step(nc.vector.tensor_scalar(place_row[:, :], LG[0:1, P:2 * P], float(ROWS - P), None, ALU.min))
            step(nc.vector.tensor_copy(tail_row[:, :], base[0:1, TPQ, :]))
            step(nc.vector.tensor_copy(pairs[:, :], pairf[0:1, 0:1]))
            dve.wait_ge(dve_s, c[0])
            nc.vector.tensor_copy(tmp4[:, 2:3], tile_no[:, :]).then_inc(table_ok, 1)
            npairs = dve.value_load(pairs[0:1, 0:1], min_val=1, max_val=40)

            def put_xt(i, s):
                dve.wait_ge(xt_ps, i + 1)
                nc.vector.tensor_copy(xT[:, s, :], bank[7][:, 0:P]).then_inc(xt_ok, 1)

            def gated(i, s):
                dve.wait_ge(act_ok, i + 1)
                nc.vector.tensor_tensor(gu[:, s, :, :].rearrange("p c t -> p (c t)"), act[:, s, :],
                                        bank[2 * s + 1][:, :], ALU.mult).then_inc(gu_ok, 1)

            put_xt(0, 0)
            put_xt(1, 1)
            gated(0, 0)
            dve.wait_ge(up_ps, 1)
            put_xt(2, 0)
            gated(1, 1)
            nc.vector.memset(tmp4[:, 3:4], 0.0).then_inc(yw_ok, 1)
            with dve.Fori(0, npairs) as j:
                for s in range(2):
                    i = j * 2 + (s + 1)
                    p_ = 1 - s
                    dve.wait_ge(up_ps, i + 1)
                    put_xt(i + 2, p_)
                    dve.wait_ge(gut_ps, i)
                    gated(i + 1, s)
                    e = dve.value_load(expert_row[0:1, bass.ds(j * 2 + s, 1)], min_val=0, max_val=E - 1)
                    dve.wait_ge(y_ps, i)
                    dve.wait_ge(added[s], j * 16 + 16)
                    nc.vector.tensor_copy(ids[:, s:s + 1], meta[:, bass.ds((j * 2 + s) * META + E, 1)].bitcast(I32)
                                          ).then_inc(ids_ok, 1)
                    dve.wait_ge(ids_ok, i)
                    nc.vector.tensor_scalar(yw[:, s, :], bank[6][:, 0:D],
                                            meta[:, bass.ds((j * 2 + s) * META + e, 1)], None,
                                            ALU.mult).then_inc(yw_ok, 1)
            dve.wait_ge(sums_in, 32)
            step(nc.vector.tensor_tensor(acc[:, 0, :, :], acc[:, 0, :, :], acc[:, 1, :, :], ALU.add))
            settled()
            step(nc.vector.tensor_tensor(acc[:, 0, :, :], acc[:, 0, :, :], x1, ALU.add))
            settled()
            for qq in range(NQ):
                stats(lambda t: acc[:, 0, qq * TPQ + t, :], st6b, mvb)
                dve.wait_ge(rstd_ok, 2 * NQ + qq + 1)
                for t in range(TPQ):
                    i = qq * TPQ + t
                    nc.vector.tensor_scalar(acc[:, 0, i, :], acc[:, 0, i, :], mvb[:, t, 0:1],
                                            rstdb[:, t:t + 1], ALU.subtract, ALU.mult).then_inc(fin_ok, 1)
                dve.wait_ge(fin_ok, (qq + 1) * TPQ)

        @block.tensor
        def _(pe):
            T = nc.tensor
            pe.wait_ge(wconv_ok, 1)
            pe.wait_ge(ident_ok, 1)
            pe.wait_ge(dma_c, 160)

            def conv(q):
                s = q % 2
                pe.wait_ge(x_in[s], 32 * (q // 2 + 1))
                if q:
                    pe.wait_ge(yct_ok, q)
                for ch in range(CH):
                    k = P if ch < 6 else RIM
                    last = T.matmul(CONV[:, :], wconv[0:k, ch, :], xcol[0:k, s, ch, :],
                                    start=(ch == 0), stop=(ch == CH - 1))
                last.then_inc(conv_ok, 1)

            def transposes(dst, src):
                for t in range(TPQ):
                    last = T.transpose(dst[:, t * P:(t + 1) * P], src(t), ident[:, :])
                return last

            tile = lambda a: (lambda t: a[:, t * P:(t + 1) * P])
            heads3 = lambda a: (lambda t: a[:, t * HEADS:(t + 1) * HEADS, :].rearrange("p h m -> p (h m)"))
            of_image = lambda a, i: a[:, :, :].rearrange("p h t -> p (h t)")[:, i:HEADS * QT:IPQ]
            conv(0)
            for q in range(NQ):
                pe.wait_ge(yct_ok, q + 1)
                if q:
                    pe.wait_ge(x1_ok, q)
                transposes(TOKM, tile(ycT)).then_inc(ytok_ok, 1)
                pe.wait_ge(yn_ok, q + 1)
                if q:
                    pe.wait_ge(vt_act, 4 * q)
                    pe.wait_ge(vt_dve, 4 * q)
                transposes(NORM, lambda t: yn[:, t, :]).then_inc(ynt_ok, 1)
                pe.wait_ge(yt_ok, q + 1)
                T.matmul(H0T[:, :], dw[:, :], yT[:, :], start=True, stop=True).then_inc(h0t_ps, 1)
                for t in range(TPQ):
                    last = T.matmul(TOKM[:, t * P:(t + 1) * P], yT[:, t * P:(t + 1) * P], dw[:, :],
                                    start=True, stop=True)
                last.then_inc(h0_ps, 1)
                pe.wait_ge(h0t_ok, q + 1)
                if q:
                    pe.wait_ge(x1t_ok, q)
                    pe.wait_ge(idx_ok, q)
                for i, (dst, done) in enumerate(((KB, k_ps), (VB, v_ps), (QB, q_ps))):
                    j = (1, 2, 0)[i]
                    T.matmul(dst[:, :], wqkv[:, j * D:(j + 1) * D], h0T[:, :], start=True,
                             stop=True).then_inc(done, 1)
                if q + 1 < NQ:
                    conv(q + 1)
                pe.wait_ge(kblk_in, 128 * (q + 1))
                pe.wait_ge(q_ok, q + 1)
                if q:
                    pe.wait_ge(st_ok, q)
                for i in range(IPQ):
                    last = T.matmul(ST[:, i * IMG:(i + 1) * IMG], of_image(kblk, i),
                                    qT[:, i:QT:IPQ], start=True, stop=True)
                last.then_inc(st_ps, 1)

                def value_fill(f):
                    if f >= 2:
                        pe.wait_ge((vt_act, vt_dve)[f % 2], 4 * q + f // 2)
                    for i in range(4 * f, 4 * f + 4):
                        last = T.transpose(VT[f % 2][:, (i % 4) * D:(i % 4 + 1) * D],
                                           of_image(vblkT, i), ident[:, :])
                    last.then_inc(vt_ps, 1)

                pe.wait_ge(vblk_in, 128 * (q + 1))
                value_fill(0)
                value_fill(1)
                pe.wait_ge(st_ok, q + 1)
                transposes(SC, tile(sT)).then_inc(sc_ps, 1)
                for f in range(2, 8):
                    value_fill(f)
                pe.wait_ge(pn_ok, q + 1)
                pe.wait_ge(k_ok, q + 1)
                transposes(PT, heads3(sc)).then_inc(pt_ps, 1)
                pe.wait_ge(pt_ok, q + 1)
                pe.wait_ge(v_ok, q + 1)
                pe.wait_ge(vt_act, 4 * q + 4)
                pe.wait_ge(vt_dve, 4 * q + 4)
                for i in range(IPQ):
                    last = T.matmul(CTX[:, i * IMG:(i + 1) * IMG], vblk[:, i, :],
                                    pT[:, i * IMG:(i + 1) * IMG], start=True, stop=True)
                last.then_inc(ctx_ps, 1)
                pe.wait_ge(ctx_ok, q + 1)
                pe.wait_ge(h0_ok, q + 1)
                for t in range(TPQ):
                    last = T.matmul(ATT[:, t * P:(t + 1) * P], ctxT[:, t * P:(t + 1) * P], wo[:, :],
                                    start=True, stop=True)
                last.then_inc(att_ps, 1)
                pe.wait_ge(x1_ok, q + 1)
                transposes(X1T, lambda t: x1[:, q * TPQ + t, :]).then_inc(x1t_ps, 1)
                pe.wait_ge(x1t_ok, q + 1)
                for t in range(TPQ):
                    last = T.matmul(LG[:, t * GR * 4:(t + 1) * GR * 4], x1T[:, t * P:(t + 1) * P], wr[:, :],
                                    start=True, stop=True)
                last.then_inc(lg_ps, 1)
                pe.wait_ge(sel_ok, q + 1)
                pe.wait_ge(ident_ok, 8)
                selv = sel[:, :, :].rearrange("p t e -> p (t e)")
                T.matmul(LG[:, 128:192], before[:, :], selv, start=True, stop=True)
                T.matmul(LG[:, 192:256], ones[:, :], selv, start=True, stop=True).then_inc(count_ps, 1)

            pe.wait_ge(tcol_ok, 1)
            T.matmul(LG[0:1, 0:P], tcol[:, 2:3], ident[:, :], start=True, stop=True)
            T.matmul(LG[0:1, P:2 * P], tcol[:, 3:4], ident[:, :], start=True, stop=True).then_inc(trow_ps, 1)
            pe.wait_ge(table_ok, 1)
            pe.wait_ge(w_in, 16 * E)
            npairs = pe.value_load(pairs[0:1, 0:1], min_val=1, max_val=40)

            def x_transpose(i, s, loads):
                pe.wait_ge(xtile_in[s], loads)
                T.transpose(bank[7][:, 0:P], xin[:, s, :], ident[:, :]).then_inc(xt_ps, 1)

            def up(i, s):
                e = pe.value_load(expert_row[0:1, bass.ds(i, 1)], min_val=0, max_val=E - 1)
                pe.wait_ge(xt_ok, i + 1)
                T.matmul(bank[2 * s][:, :], xT[:, s, :], wall[:, bass.ds(e * WEXP, HID)], start=True, stop=True)
                T.matmul(bank[2 * s + 1][:, :], xT[:, s, :], wall[:, bass.ds(e * WEXP + HID, HID)],
                         start=True, stop=True).then_inc(up_ps, 1)

            def hidden_transpose(i, s):
                pe.wait_ge(gu_ok, i + 1)
                for c4 in range(HC):
                    last = T.transpose(bank[4 + s][:, c4 * P:(c4 + 1) * P], gu[:, s, c4, :], ident[:, :])
                last.then_inc(gut_ps, 1)

            def down(i, s):
                e = pe.value_load(expert_row[0:1, bass.ds(i, 1)], min_val=0, max_val=E - 1)
                pe.wait_ge(gut_ok, i + 1)
                for c4 in range(HC):
                    last = T.matmul(bank[6][:, 0:D], guT[:, s, c4, :],
                                    wall[:, bass.ds(e * WEXP + 2 * HID + c4 * D, D)],
                                    start=(c4 == 0), stop=(c4 == HC - 1))
                last.then_inc(y_ps, 1)

            x_transpose(0, 0, 32)
            pe.wait_ge(xt_ok, 1)
            x_transpose(1, 1, 32)
            up(0, 0)
            up(1, 1)
            pe.wait_ge(xt_ok, 2)
            x_transpose(2, 0, 64)
            hidden_transpose(0, 0)
            with pe.Fori(0, npairs) as j:
                for s in range(2):
                    i = j * 2 + (s + 1)
                    pe.wait_ge(gu_ok, i)
                    up(i + 1, s)
                    pe.wait_ge(xt_ok, i + 2)
                    x_transpose(i + 2, 1 - s, j * 32 + 64 + 32 * s)
                    hidden_transpose(i, 1 - s)
                    pe.wait_ge(yw_ok, i)
                    down(i - 1, s)


def host_layout(x, conv_w):
    import numpy as np
    x = np.asarray(x)
    w = np.asarray(conv_w)
    B = x.shape[0]
    S = 16
    xp = np.zeros((B, 66, 66, 3), x.dtype)
    xp[:, 1:65, 1:65] = x
    main = x.reshape(NQ, IPQ, 4, S, 4, S, 3).transpose(3, 5, 6, 0, 2, 4, 1).reshape(6, P, NQ, QT)
    main = np.ascontiguousarray(main.transpose(2, 1, 0, 3))
    cols = np.stack([xp[:, 1:65, 0:64:S], xp[:, 1:65, 17:66:S]])
    cols = cols.reshape(2, NQ, IPQ, 4, S, 4, 3).transpose(0, 4, 6, 1, 3, 5, 2).reshape(RIM, NQ, QT)
    rows = np.stack([xp[:, 0:64:S, 1:65], xp[:, 17:66:S, 1:65]])
    rows = rows.reshape(2, NQ, IPQ, 4, 4, S, 3).transpose(0, 5, 6, 1, 3, 4, 2).reshape(RIM, NQ, QT)
    rim = np.ascontiguousarray(np.stack([cols, rows]).transpose(2, 1, 0, 3))
    c, r, l, d, u = (w[:, :, 3 * i:3 * i + 3] for i in range(5))
    t = np.zeros((5, S, S, 3, D), w.dtype)
    t[0] = c
    t[1][:, :-1] = r[:, 1:]
    t[2][:, 1:] = l[:, :-1]
    t[3][:-1] = d[1:]
    t[4][1:] = u[:-1]
    taps = np.ascontiguousarray(t.reshape(5, 6, P, D).transpose(2, 0, 1, 3))
    wrim = np.stack([np.stack([r[:, 0], l[:, S - 1]]).reshape(RIM, D),
                     np.stack([d[0], u[S - 1]]).reshape(RIM, D)])
    return main, rim, taps, np.ascontiguousarray(wrim.transpose(1, 0, 2))


def kernel(**inputs):
    import numpy as np
    import concourse.bacc as bacc
    from concourse.bass_utils import run_bass_kernel_spmd

    g = {k: np.asarray(v) for k, v in inputs.items()}
    main, rim, taps, wrim = host_layout(g["x"], g["L0_tok_conv_w"])
    wroute = np.concatenate([g["L0_ffn_Wr"], g["L0_ffn_Wgate"].transpose(1, 0, 2).reshape(D, 16)], axis=1)
    broute = np.concatenate([g["L0_ffn_br"], g["L0_ffn_bgate"].reshape(16)])
    arrays = {
        "xmain": main, "xrim": rim, "taps": taps, "wrim": wrim,
        "conv_b": g["L0_tok_conv_b"], "gamma": g["L0_tok_gamma"], "beta": g["L0_tok_beta"],
        "dense_w": g["L0_tok_dense_w"], "dense_b": g["L0_tok_dense_b"],
        "wqkv_t": g["L0_attn_w_qkv"].T, "wo_t": g["L0_attn_w_o"].T,
        "wroute": wroute, "broute": broute,
        "wexp": np.concatenate([g["L0_ffn_W1"], g["L0_ffn_W3"],
                                g["L0_ffn_W2"].reshape(E, HC, P, D).transpose(0, 2, 1, 3).reshape(E, P, HC * D)],
                               axis=2),
    }
    arrays = {k: np.ascontiguousarray(v) for k, v in arrays.items()}
    nc = bacc.Bacc("TRN2", target_bir_lowering=False, num_devices=1)
    args = [nc.dram_tensor(f"in_{k}", v.shape, mybir.dt.from_np(v.dtype), kind="ExternalInput").ap()
            for k, v in arrays.items()]
    args.append(nc.dram_tensor("lists", (ROWS, ROW), F32, kind="Internal").ap())
    for name in ("sums_even", "sums_odd"):
        args.append(nc.dram_tensor(name, (TOKENS + P, D), F32, kind="Internal").ap())
    out = nc.dram_tensor("out", (P, TILES, D), F32, kind="ExternalOutput").ap()
    build_program(nc, *args, out)
    r = run_bass_kernel_spmd(nc, [{f"in_{k}": v for k, v in arrays.items()}], core_ids=[0])
    got = r.results[0]["out"]
    got = got.transpose(1, 0, 2).reshape(NQ, IMG, IPQ, D).transpose(0, 2, 1, 3)
    return np.ascontiguousarray(got).reshape(NQ * IPQ, IMG, D)
```

```python
from contextlib import ExitStack

import concourse.bass as bass
from concourse import mybir

ALU = mybir.AluOpType
ACT = mybir.ActivationFunctionType
AX = mybir.AxisListType
F32 = mybir.dt.float32
I32 = mybir.dt.int32
U32 = mybir.dt.uint32

P = 128
D = 128
TOKENS = 2048
QT = 512
NQ = TOKENS // QT
TPQ = QT // P
IMG = 16
IPQ = QT // IMG
HEADS = 8
DK = D // HEADS
SCALE = DK ** -0.5
NB = IPQ // 4
G = 4
EPG = 4
E = G * EPG
GR = G + 1
HID = 512
HC = HID // P
TILES = TOKENS // P
CH = 8
RIM = 96
CAP = TOKENS + P
DUMMY = E * CAP
ROWS = DUMMY + 4 * P
META = E + 1
ROW = D + META
WEXP = 2 * HID + HC * D
MAXT = P
EARLY_STEPS = 8
EARLY = EARLY_STEPS + 2
LAST_DVE = 5
FIRST_SCATTERS = 12
K = 4
U = 4
TAILS_PER_STEP = (2, 2, 2, 0)
ACT_TAILS = E - EARLY_STEPS // U * sum(TAILS_PER_STEP)
MIN_BODIES = TILES // U
MAX_BODIES = (EARLY + K * TILES + E - 1 + U - 1) // U
SKIP = 4 * ROWS
TOK_EPS = 1e-3
LN_EPS = 1e-5


def build_program(nc, xmain, xrim, taps, wrim, conv_b, gamma, beta, dense_w, dense_b, wqkv_t,
                  wo_t, wroute, broute, wexp,
                  lists, sums_even, sums_odd, out):
    sums = [sums_even, sums_odd]
    ctx = ExitStack()
    with ctx:
        def sb(name, shape, dt=F32):
            return ctx.enter_context(nc.sbuf_tensor(name, shape, dt))

        def sem(name):
            return ctx.enter_context(nc.semaphore(name))

        bank = [ctx.enter_context(nc.psum_tensor(f"bank{i}", [P, 512], F32)) for i in range(8)]
        QB = bank[0]
        CONV = [bank[0], bank[2], bank[0], bank[0]]
        TOKM, ATT = bank[1], bank[1]
        VT, CTX = bank[2:4], bank[2:4]
        SC, KB, VB = bank[4:6], bank[4], bank[5]
        PT, X1T, CNT = bank[6], bank[6], bank[6]
        NORM, H0T, LG, CTXT = bank[7], bank[7], bank[7], bank[7]

        ident = sb("ident", [P, P])
        wall = sb("wall", [P, E * WEXP])
        later = E // 2 * WEXP
        xcol = wall[:, later:later + 2 * CH * QT].rearrange("p (s c t) -> p s c t", s=2, c=CH)
        tapsum = wall[:, later + 2 * CH * QT:later + 2 * CH * QT + 30 * D].rearrange(
            "p (a c d) -> p a c d", a=5, c=6)
        wconv = sb("wconv", [P, CH, D])
        convb = sb("convb", [P, 1])
        gam = sb("gam", [P, 1])
        bet = sb("bet", [P, 1])
        dw = sb("dw", [P, D])
        dbcol = sb("dbcol", [P, 1])
        dbrow = sb("dbrow", [P, D])
        wqkv = sb("wqkv", [P, 3 * D])
        wo = sb("wo", [P, D])
        wr = sb("wr", [P, GR * 4])
        br = sb("br", [P, GR * 4])
        ycT = sb("ycT", [P, 2, QT])
        st6 = sb("st6", [P, TPQ, 6])
        mv = sb("mv", [P, TPQ, 2])
        rstd = sb("rstd", [P, TPQ])
        halved = sb("halved", [P, TILES], I32)
        newton = sb("newton", [P, TILES])
        st6b = sb("st6b", [P, TILES, 6])
        mvb = sb("mvb", [P, TILES, 2])
        rstdb = sb("rstdb", [P, TILES])
        shift = sb("shift", [P, TILES])
        veps = sb("veps", [P, TILES])
        yn = sb("yn", [P, TPQ, D])
        yT = sb("yT", [P, 2, QT])
        pshift = sb("pshift", [P, TPQ])
        h0T = sb("h0T", [P, QT])
        qT = sb("qT", [P, QT + IMG])
        kT = sb("kT", [P, QT])
        vT = sb("vT", [P, QT])
        kblk = sb("kblk", [P, HEADS, QT])
        vblkT = sb("vblkT", [P, HEADS, QT])
        vblk = sb("vblk", [P, IPQ, D])
        sc = sb("sc", [P, NB * HEADS, IMG])
        ctxs = sc[:, :, :].rearrange("p (j h) m -> p j (h m)", h=HEADS)
        smax = sb("smax", [P, NB * HEADS])
        ssum = sb("ssum", [P, NB * HEADS])
        srec = sb("srec", [P, NB * HEADS])
        pT = sb("pT", [P, QT + IMG])
        ctxT = sb("ctxT", [P, QT])
        res = sb("res", [P, TPQ, D])
        rows = sb("rows", [P, TILES, ROW])
        x1 = rows[:, :, 0:D]
        x1T = sb("x1T", [P, QT])
        R = TPQ * GR
        lg = sb("lg", [P, R, 4])
        lmax = sb("lmax", [P, R])
        lsh = sb("lsh", [P, R, 4])
        lex = sb("lex", [P, R, 4])
        lsum = sb("lsum", [P, R])
        lrec = sb("lrec", [P, R])
        gp = sb("gp", [P, R, 4])
        gt = sb("gt", [P, R, 4, 4])
        top2 = sb("top2", [P, R, 4])
        rank = sb("rank", [P, R, 4])
        first = sb("first", [P, R, 4])
        second = sb("second", [P, R, 4])
        psec = sb("psec", [P, R, 4])
        cum = sb("cum", [P, R])
        keep2 = sb("keep2", [P, R])
        kept = sb("kept", [P, R, 4])
        mask = sb("mask", [P, R, 4])
        mp = sb("mp", [P, R, 4])
        msum = sb("msum", [P, R])
        mrec = sb("mrec", [P, R])
        wn = sb("wn", [P, R, 4])
        sel = sb("sel", [P, TPQ, E])
        before = sb("before", [P, P])
        ones = sb("ones", [P, P])
        base = sb("base", [P, TILES + 1, E])
        pos = sb("pos", [P, TPQ, E])
        pick = sb("pick", [P, K, TPQ, E])
        picked = sb("picked", [P, K, TPQ, E])
        taken = sb("taken", [P, K, TPQ])
        place = sb("place", [P, K, TPQ])
        idx = sb("idx", [P, NQ, K * TPQ], I32)
        tile_no = sb("tile_no", [P, 1])
        late_no = sb("late_no", [P, 1])
        firsts = sb("firsts", [P, E])
        steps16 = sb("steps16", [P, TILES + 1])
        ntl = sb("ntl", [P, E])
        early = sb("early", [P, E + 1])
        early_step = sb("early_step", [P, E])
        full = sb("full", [P, E])
        ngt = sb("ngt", [P, E, TILES + 1])
        ends = sb("ends", [P, E])
        past = sb("past", [P, E])
        pastn = sb("pastn", [P, E])
        tcol = sb("tcol", [P, 4])
        tmp4 = sb("tmp4", [P, 4])
        mark = sb("mark", [1, 1])
        waited = sb("waited", [1, 2])
        expert_early = sb("expert_early", [1, EARLY], I32)
        place_early = sb("place_early", [1, EARLY], I32)
        expert_row = sb("expert_row", [1, MAXT], I32)
        place_row = sb("place_row", [1, MAXT], I32)
        tail_row = sb("tail_row", [1, E], I32)
        bodies_i = sb("bodies_i", [1, 1], I32)
        bodies_f = sb("bodies_f", [1, 2])
        xin = kblk[:, 0, 0:2 * P].rearrange("p (s d) -> p s d", s=2)
        xT = kblk[:, 1, 0:2 * P].rearrange("p (s d) -> p s d", s=2)
        yw = kblk[:, 2, 0:2 * D].rearrange("p (s d) -> p s d", s=2)
        filler = sb("filler", [P, ROW])
        meta = vblk[:, 0:13, :].rearrange("p a b -> p (a b)")[:, 0:(U * MAX_BODIES + 3) * META]
        act = vblkT[:, 0:2, :]
        gu = vblkT[:, 2:4, :].rearrange("p s (c t) -> p s c t", t=P)
        guT = vblkT[:, 4:6, :].rearrange("p s (c t) -> p s c t", t=P)
        ids = sb("ids", [P, 2], I32)
        warm = sb("warm", [P, 1])
        acc = wall[:, 0:2 * TILES * D].rearrange("p (a t d) -> p a t d", a=2, t=TILES)

        taps_in = [sem("taps_in0"), sem("taps_in1")]
        rim_in = sem("rim_in")
        x_first = sem("x_first")
        dma_c = sem("dma_c")
        x_in = [sem("x_in0"), sem("x_in1")]
        zeros = sem("zeros")
        ident_ok = sem("ident_ok")
        pool_c = sem("pool_c")
        wconv_ok = sem("wconv_ok")
        conv_ok = sem("conv_ok")
        yct_ok = sem("yct_ok")
        ytok_ok = sem("ytok_ok")
        yn_ok = sem("yn_ok")
        ynt_ok = sem("ynt_ok")
        yt_ok = sem("yt_ok")
        h0t_ps = sem("h0t_ps")
        pstat_ok = sem("pstat_ok")
        res_ok = sem("res_ok")
        astat_ok = sem("astat_ok")
        x1_dve = sem("x1_dve")
        h0t_ok = sem("h0t_ok")
        q_ps = sem("q_ps")
        k_ps = sem("k_ps")
        v_ps = sem("v_ps")
        q_ok = sem("q_ok")
        k_ok = sem("k_ok")
        v_ok = sem("v_ok")
        kblk_in = sem("kblk_in")
        vblk_in = sem("vblk_in")
        vt_ps = sem("vt_ps")
        vt_act = sem("vt_act")
        sc_ps = sem("sc_ps")
        sh_ok = sem("sh_ok")
        exp_ok = sem("exp_ok")
        pn_ok = sem("pn_ok")
        pt_ps = sem("pt_ps")
        pt_ok = sem("pt_ok")
        ctx_ps = sem("ctx_ps")
        ctx_ok = sem("ctx_ok")
        att_ps = sem("att_ps")
        x1_ok = sem("x1_ok")
        x1t_ps = sem("x1t_ps")
        x1t_ok = sem("x1t_ok")
        lg_ps = sem("lg_ps")
        lsh_ok = sem("lsh_ok")
        lex_ok = sem("lex_ok")
        dve_s = sem("dve_s")
        w_in = sem("w_in")
        zeroed = sem("zeroed")
        kept_in = sem("kept_in")
        filler_ok = sem("filler_ok")
        sel_ok = sem("sel_ok")
        count_ps = sem("count_ps")
        idx_ok = sem("idx_ok")
        scattered = sem("scattered")
        scattered_last = sem("scattered_last")
        tail_row_ok = sem("tail_row_ok")
        early_ok = sem("early_ok")
        tcol_ok = sem("tcol_ok")
        trow_ps = sem("trow_ps")
        table_ok = sem("table_ok")
        tails = sem("tails")
        xtile_in = [sem("xtile_in0"), sem("xtile_in1")]
        xt_ps = sem("xt_ps")
        xt_ok = sem("xt_ok")
        yw_ok = sem("yw_ok")
        added = [sem("added0"), sem("added1")]
        sums_in = [sem(f"sums_in{h}") for h in range(4)]
        summed = [sem("summed0"), sem("summed1")]
        fin_act = sem("fin_act")
        shift_ok = sem("shift_ok")
        ctx_act = sem("ctx_act")
        ctxt_ps = sem("ctxt_ps")
        up_ps = sem("up_ps")
        act_ok = sem("act_ok")
        gu_ok = sem("gu_ok")
        gut_ps = sem("gut_ps")
        gut_ok = sem("gut_ok")
        y_ps = sem("y_ps")
        ids_ok = sem("ids_ok")
        carried = sem("carried")
        fin_ok = sem("fin_ok")
        out_done = sem("out_done")

        block = ctx.enter_context(nc.Block())

        @block.sync
        def _(sp):
            for h in range(2):
                sp.dma_start(tapsum[:, :, 3 * h:3 * h + 3, :], taps[:, :, 3 * h:3 * h + 3, :]).then_inc(taps_in[h], 16)
            sp.dma_start(xcol[:, 0, 0:3, :], xmain[0, :, 0:3, :]).then_inc(x_first, 16)
            sp.dma_start(xcol[:, 0, 3:6, :], xmain[0, :, 3:6, :]).then_inc(x_in[0], 16)
            sp.dma_start(xcol[0:RIM, 0, 6:8, :], xrim[0]).then_inc(x_in[0], 16)
            sp.dma_start(wconv[0:RIM, 6:8, :], wrim).then_inc(rim_in, 16)

            def load_x(q, slot):
                sp.dma_start(xcol[:, slot, 0:6, :], xmain[q]).then_inc(x_in[slot], 16)
                sp.dma_start(xcol[0:RIM, slot, 6:8, :], xrim[q]).then_inc(x_in[slot], 16)

            for dst, src in ((dw, dense_w), (wqkv, wqkv_t), (wo, wo_t)):
                sp.dma_start(dst[:, :], src).then_inc(dma_c, 16)
            load_x(1, 1)

            def load_experts(first, last):
                for e in range(first, last):
                    sp.dma_start(wall[:, e * WEXP:(e + 1) * WEXP], wexp[e]).then_inc(w_in, 16)

            load_experts(0, 2)
            for q in range(2, NQ):
                sp.wait_ge(conv_ok, q - 1)
                load_x(q, q % 2)

            def blocks(q):
                sp.wait_ge(zeros, 2)
                sp.wait_ge(k_ok, q + 1)
                sp.wait_ge(sc_ps, q)
                for h in range(HEADS):
                    sp.dma_start(kblk[DK * h:DK * (h + 1), h, :],
                                 kT[DK * h:DK * (h + 1), :]).then_inc(kblk_in, 16)
                sp.wait_ge(v_ok, q + 1)
                sp.wait_ge(vt_ps, 8 * q)
                for h in range(HEADS):
                    sp.dma_start(vblkT[DK * h:DK * (h + 1), h, :],
                                 vT[DK * h:DK * (h + 1), :]).then_inc(vblk_in, 16)

            def keep_rows(q):
                sp.wait_ge(x1_ok, q + 1)
                if q == NQ - 1:
                    sp.wait_ge(x1_dve, 1)
                sp.dma_start(sums_even[0:TOKENS, :].rearrange("(p t) d -> p t d", t=TILES)[:, q * TPQ:(q + 1) * TPQ, :],
                             rows[:, q * TPQ:(q + 1) * TPQ, 0:D]).then_inc(kept_in, 16)

            blocks(0)
            load_experts(2, 6)
            blocks(1)
            sp.wait_ge(filler_ok, 2)
            sp.dma_start(sums_odd.rearrange("(n p) d -> p n d", p=P),
                         filler[:, 0:D].unsqueeze(1).to_broadcast([P, TILES + 1, D])).then_inc(zeroed, 16)
            sp.dma_start(sums_even[TOKENS:TOKENS + P, :], filler[:, 0:D]).then_inc(zeroed, 16)
            sp.dma_start(lists[DUMMY:ROWS, :].rearrange("(n p) d -> p n d", p=P),
                         filler[:, :].unsqueeze(1).to_broadcast([P, 4, ROW])).then_inc(zeroed, 16)
            load_experts(6, 8)
            sp.wait_ge(conv_ok, NQ)
            load_experts(8, 11)
            keep_rows(0)
            blocks(2)
            load_experts(11, E)
            keep_rows(1)
            blocks(3)
            keep_rows(2)
            def load_tile(i, s, table):
                at = sp.value_load(table[0:1, bass.ds(i, 1)], min_val=0, max_val=ROWS - P)
                sp.dma_start(xin[:, s, :], lists[bass.ds(at, P), 0:D]).then_inc(xtile_in[s], 16)
                sp.dma_start(meta[:, bass.ds(i * META, META)], lists[bass.ds(at, P), D:ROW]).then_inc(xtile_in[s], 16)

            sp.wait_ge(early_ok, 1)
            sp.wait_ge(scattered, 16 * K * TPQ * (NQ - 1))
            load_tile(0, 0, place_early)
            load_tile(1, 1, place_early)
            keep_rows(NQ - 1)

            def fill_tail(e):
                at = sp.value_load(tail_row[0:1, bass.ds(e, 1)], min_val=0, max_val=DUMMY - P)
                sp.dma_start(lists[bass.ds(at, P), :], filler[:, :]).then_inc(tails, 16)

            sp.wait_ge(tail_row_ok, 1)

            def loads(j, table, tiles=range(2, U + 2), tails_too=False):
                for u in (t - 2 for t in tiles):
                    sp.wait_ge(xt_ps, j * U + (u + 1))
                    load_tile(j * U + (u + 2), u % 2, table)
                    if tails_too:
                        for n in range(TAILS_PER_STEP[u]):
                            fill_tail(j * sum(TAILS_PER_STEP) + (ACT_TAILS + sum(TAILS_PER_STEP[:u]) + n))

            with sp.Fori(0, EARLY_STEPS // U) as j:
                loads(j, place_early, tails_too=True)
            sp.wait_ge(table_ok, 1)
            sp.wait_ge(scattered_last, 16 * K * TPQ)
            sp.wait_ge(tails, 16 * E)
            rest = sp.value_load(bodies_i[0:1, 0:1], min_val=MIN_BODIES - 1, max_val=MAX_BODIES - 1)
            with sp.Fori(EARLY_STEPS // U, rest) as j:
                loads(j, place_row)
            loads(rest, place_row, range(2, U))
            for a in range(2):
                sp.wait_ge(added[a], rest * (8 * U) + (8 * U + 16))
                for h in range(4):
                    sp.dma_start(acc[:, a, 4 * h:4 * h + 4, :],
                                 sums[a][0:TOKENS, :].rearrange("(p t) d -> p t d", t=TILES)[:, 4 * h:4 * h + 4, :]
                                 ).then_inc(sums_in[h], 16)
            H = TILES // 2
            for h in range(2):
                sp.wait_ge(fin_ok, h + 1)
                sp.wait_ge(fin_act, h + 1)
                sp.dma_start(out[:, h * H:(h + 1) * H, :], acc[:, 0, h * H:(h + 1) * H, :]).then_inc(out_done, 16)
            sp.wait_ge(out_done, 32)

        @block.gpsimd
        def _(pool):
            pool.memset(ident[:, :], 0.0).then_inc(pool_c, 1)
            pool.wait_ge(pool_c, 1)
            pool.affine_select(out=ident[:, :], in_=ident[:, :], compare_op=ALU.not_equal, fill=1.0,
                               base=0, pattern=[[-1, P]], channel_multiplier=1).then_inc(ident_ok, 1)
            pool.memset(filler[:, :], 0.0).then_inc(filler_ok, 1)
            pool.wait_ge(filler_ok, 1)
            pool.iota(filler[:, ROW - 1:ROW].bitcast(I32), pattern=[[0, 1]], base=TOKENS,
                      channel_multiplier=1).then_inc(filler_ok, 1)
            pool.iota(rows[:, :, ROW - 1:ROW].bitcast(I32), pattern=[[1, TILES], [0, 1]], base=0,
                      channel_multiplier=TILES).then_inc(ident_ok, 1)
            pool.memset(ones[:, :], 1.0).then_inc(ident_ok, 1)
            pool.memset(before[:, :], 1.0).then_inc(pool_c, 1)
            pool.wait_ge(pool_c, 2)
            pool.affine_select(out=before[:, :], in_=before[:, :], compare_op=ALU.is_gt, fill=0.0,
                               base=0, pattern=[[1, P]], channel_multiplier=-1).then_inc(ident_ok, 1)
            for dst, pat, start, mul in ((tile_no[:, :], [[0, 1]], 0, 1), (late_no[:, :], [[0, 1]], -EARLY, 1),
                                         (firsts[:, :], [[CAP, E]], 0, 0),
                                         (steps16[:, :], [[P, TILES + 1]], 0, 0)):
                pool.iota(dst, pattern=pat, base=start, channel_multiplier=mul,
                          allow_small_or_imprecise_dtypes=True).then_inc(ident_ok, 1)
            pool.memset(kblk[:, :, :], 0.0).then_inc(zeros, 1)
            pool.memset(vblkT[:, :, :], 0.0).then_inc(zeros, 1)
            pool.memset(qT[:, QT:QT + IMG], 0.0).then_inc(zeros, 1)
            pool.memset(pT[:, QT:QT + IMG], 0.0).then_inc(zeros, 1)
            def scatter(q, n, done):
                t = n % TPQ
                pool.indirect_dma_start(
                    out=lists, out_offset=bass.IndirectOffsetOnAxis(
                        ap=idx[:, q, n:n + 1].bitcast(U32), axis=0),
                    in_=rows[:, q * TPQ + t, :], in_offset=None,
                    bounds_check=ROWS - 1, oob_is_err=False).then_inc(done, 16)

            for q in range(NQ - 1):
                pool.wait_ge(idx_ok, q + 1)
                for n in range(K * TPQ):
                    scatter(q, n, scattered)
                if q == NQ - 2:
                    pool.wait_ge(zeroed, 48)
                    for s in range(2):
                        pool.indirect_dma_start(
                            out=sums[s], out_offset=bass.IndirectOffsetOnAxis(
                                ap=filler[:, ROW - 1:ROW].bitcast(U32), axis=0),
                            in_=filler[:, 0:D], in_offset=None, bounds_check=TOKENS + P - 1,
                            compute_op=ALU.add).then_inc(added[s], 16)
            pool.memset(mark[:, :], 0.0).then_inc(carried, 1)
            pool.wait_ge(idx_ok, NQ)
            for n in range(FIRST_SCATTERS):
                scatter(NQ - 1, n, scattered_last)
            pool.wait_ge(kept_in, 16 * NQ)

            def add_results(j, u):
                s = u % 2
                pool.wait_ge(yw_ok, j * U + (u + 2))
                pool.wait_ge(added[s], j * (8 * U) + (u // 2 * 16 + 16))
                pool.wait_ge(carried, j * U + (u + 1))
                pool.tensor_tensor(waited[:, s:s + 1], mark[:, :], mark[:, :], ALU.add).then_inc(carried, 1)
                pool.indirect_dma_start(
                    out=sums[s], out_offset=bass.IndirectOffsetOnAxis(ap=ids[:, s:s + 1].bitcast(U32), axis=0),
                    in_=yw[:, s, :], in_offset=None, bounds_check=TOKENS + P - 1,
                    compute_op=ALU.add).then_inc(added[s], 16)

            for i in range(EARLY_STEPS):
                for n in range(FIRST_SCATTERS + 2 * i, min(FIRST_SCATTERS + 2 * i + 2, K * TPQ)):
                    scatter(NQ - 1, n, scattered_last)
                add_results(i // U, i % U)
            pool.wait_ge(table_ok, 1)
            rest = pool.value_load(bodies_i[0:1, 0:1], min_val=MIN_BODIES - 1, max_val=MAX_BODIES - 1)
            with pool.Fori(EARLY_STEPS // U, rest) as j:
                for u in range(U):
                    add_results(j, u)
            for u in range(U):
                add_results(rest, u)
            for h in range(2, 4):
                pool.wait_ge(sums_in[h], 32)
                pool.tensor_tensor(acc[:, 0, 4 * h:4 * h + 4, :], acc[:, 0, 4 * h:4 * h + 4, :],
                                   acc[:, 1, 4 * h:4 * h + 4, :], ALU.add).then_inc(summed[h - 2], 1)

        @block.scalar
        def _(ac):
            for dst, src in ((convb[:, :], conv_b), (gam[:, :], gamma), (bet[:, :], beta),
                             (dbcol[:, :], dense_b)):
                ac.dma_start(dst, src.rearrange("(p a) -> p a", a=1)).then_inc(dma_c, 16)
            ac.dma_start(wr[:, :], wroute).then_inc(dma_c, 16)
            ac.dma_start(dbrow[:, :], dense_b.partition_broadcast(P)).then_inc(dma_c, 16)
            ac.dma_start(br[:, :], broute.partition_broadcast(P)).then_inc(dma_c, 16)
            ac.wait_ge(ident_ok, 1)
            ac.activation(warm[:, 0:1], ident[:, 0:1], ACT.Exp)
            ac.wait_ge(dma_c, 160)

            def conv_out(q):
                ac.wait_ge(conv_ok, q + 1)
                if q > 1:
                    ac.wait_ge(ytok_ok, q - 1)
                ac.activation(ycT[:, q % 2, :], CONV[q][:, :], ACT.Identity, bias=convb[:, 0:1]).then_inc(yct_ok, 1)

            def patch_normed(q):
                ac.wait_ge(pstat_ok, q + 1)
                for t in range(TPQ):
                    last = ac.activation(yn[:, t, :], TOKM[:, t * P:(t + 1) * P], ACT.Identity,
                                         bias=pshift[:, t:t + 1], scale=rstd[:, t:t + 1])
                last.then_inc(yn_ok, 1)

            def attention_normed(q, tiles):
                ac.wait_ge(astat_ok, q + 1)
                for t in tiles:
                    last = ac.activation(x1[:, q * TPQ + t, :], res[:, t, :], ACT.Identity,
                                         bias=shift[:, t:t + 1], scale=rstdb[:, t:t + 1])
                last.then_inc(x1_ok, 1)

            def x1_turned_out(q):
                ac.wait_ge(x1t_ps, q + 1)
                ac.activation(x1T[:, :], X1T[:, :], ACT.Copy).then_inc(x1t_ok, 1)

            def normed(q):
                ac.wait_ge(ynt_ok, q + 1)
                ac.activation(yT[:, q % 2, :], NORM[:, :], ACT.Identity, bias=bet[:, 0:1],
                              scale=gam[:, 0:1]).then_inc(yt_ok, 1)

            def embedded(q):
                ac.wait_ge(h0t_ps, q + 1)
                ac.activation(h0T[:, :], H0T[:, :], ACT.Identity, bias=dbcol[:, 0:1]).then_inc(h0t_ok, 1)

            def keys_out(q):
                ac.wait_ge(k_ps, q + 1)
                if q:
                    ac.wait_ge(kblk_in, 128 * q)
                ac.activation(kT[:, :], KB[:, :], ACT.Copy).then_inc(k_ok, 1)

            def values_out(q):
                ac.wait_ge(v_ps, q + 1)
                if q:
                    ac.wait_ge(vblk_in, 128 * q)
                ac.activation(vT[:, :].rearrange("p (m i) -> p i m", i=IPQ),
                              VB[:, :].rearrange("p (i m) -> p i m", m=IMG), ACT.Copy).then_inc(v_ok, 1)

            def queries_out(q):
                ac.wait_ge(q_ps, q + 1)
                ac.activation(qT[:, 0:QT], QB[:, :], ACT.Copy, scale=SCALE).then_inc(q_ok, 1)

            def values(q, fills):
                for f in fills:
                    ac.wait_ge(vt_ps, 8 * q + f + 1)
                    ac.activation(vblk[:, 4 * f:4 * f + 4, :], VT[f % 2][:, :].rearrange("p (i d) -> p i d", d=D),
                                  ACT.Copy).then_inc(vt_act, 1)

            conv_out(0)
            patch_normed(0)
            conv_out(1)
            normed(0)
            embedded(0)
            keys_out(0)
            values_out(0)
            queries_out(0)
            patch_normed(1)
            conv_out(2)
            for q in range(NQ):
                values(q, (0, 1))
                if q:
                    attention_normed(q - 1, range(TPQ))
                else:
                    values(q, (2, 3))
                ac.wait_ge(sh_ok, q + 1)
                ac.activation(sc[:, :, :], sc[:, :, :], ACT.Exp).then_inc(exp_ok, 1)
                if q:
                    values(q, (2, 3))
                    x1_turned_out(q - 1)
                values(q, (4, 5, 6, 7))
                if q and q + 1 < NQ:
                    patch_normed(q + 1)
                if q:
                    ac.wait_ge(lsh_ok, q)
                    ac.activation(lex[:, :, :], lsh[:, :, :], ACT.Exp).then_inc(lex_ok, 1)
                if q + 1 < NQ:
                    normed(q + 1)
                    embedded(q + 1)
                if q == 1:
                    conv_out(NQ - 1)
                ac.wait_ge(pt_ps, q + 1)
                ac.activation(pT[:, 0:QT], PT[:, :], ACT.Copy).then_inc(pt_ok, 1)
                if q + 1 < NQ:
                    keys_out(q + 1)
                for h in range(2):
                    ac.wait_ge(ctx_ps, 2 * q + h + 1)
                    ac.activation(ctxs[:, 4 * h:4 * h + 4, :], CTX[h][:, :].rearrange("p (j d) -> p j d", d=D),
                                  ACT.Copy).then_inc(ctx_act, 1)
                if q + 1 < NQ:
                    values_out(q + 1)
                ac.wait_ge(ctxt_ps, q + 1)
                ac.activation(ctxT[:, :], CTXT[:, :], ACT.Copy).then_inc(ctx_ok, 1)
                if q + 1 < NQ:
                    queries_out(q + 1)
            attention_normed(NQ - 1, (2, 3))
            x1_turned_out(NQ - 1)
            ac.wait_ge(lsh_ok, NQ)
            ac.activation(lex[:, :, :], lsh[:, :, :], ACT.Exp).then_inc(lex_ok, 1)
            ac.activation(warm[:, 0:1], convb[:, 0:1], ACT.Silu)

            def silu_of(n, s):
                ac.wait_ge(up_ps, n + 1)
                ac.activation(act[:, s, :], bank[2 * s][:, :], ACT.Silu).then_inc(act_ok, 1)

            def gut_of(n, s):
                ac.wait_ge(gut_ps, n + 1)
                ac.activation(guT[:, s, :, :], bank[4 + s][:, :].rearrange("p (c t) -> p c t", t=P),
                              ACT.Copy).then_inc(gut_ok, 1)

            ac.wait_ge(tail_row_ok, 1)
            for e in range(ACT_TAILS):
                at = ac.value_load(tail_row[0:1, bass.ds(e, 1)], min_val=0, max_val=DUMMY - P)
                ac.dma_start(lists[bass.ds(at, P), :], filler[:, :]).then_inc(tails, 16)
            silu_of(0, 0)
            silu_of(1, 1)
            gut_of(0, 0)

            def hidden(j, last=False):
                for u in range(U):
                    if not last or u + 2 < U:
                        silu_of(j * U + (u + 2), u % 2)
                    if not last or u + 1 < U:
                        gut_of(j * U + (u + 1), 1 - u % 2)

            with ac.Fori(0, EARLY_STEPS // U) as j:
                hidden(j)
            ac.wait_ge(table_ok, 1)
            rest = ac.value_load(bodies_i[0:1, 0:1], min_val=MIN_BODIES - 1, max_val=MAX_BODIES - 1)
            with ac.Fori(EARLY_STEPS // U, rest) as j:
                hidden(j)
            hidden(rest, last=True)
            ac.wait_ge(shift_ok, 1)
            for h in range(2):
                for t in range(h * 8 + LAST_DVE, h * 8 + 8):
                    last = ac.activation(acc[:, 0, t, :], acc[:, 0, t, :], ACT.Identity, bias=shift[:, t:t + 1],
                                         scale=rstdb[:, t:t + 1])
                last.then_inc(fin_act, 1)

        @block.vector
        def _(dve):
            c = [0]

            def step(inst):
                inst.then_inc(dve_s, 1)
                c[0] += 1

            def settled():
                dve.wait_ge(dve_s, c[0])

            for h in range(2):
                dve.wait_ge(taps_in[h], 16)
                tp = [tapsum[:, i, 3 * h:3 * h + 3, :] for i in range(5)]
                wc = wconv[:, 3 * h:3 * h + 3, :]
                step(nc.vector.tensor_tensor(wc, tp[0], tp[1], ALU.add))
                step(nc.vector.tensor_tensor(tp[2], tp[2], tp[3], ALU.add))
                settled()
                step(nc.vector.tensor_tensor(wc, wc, tp[4], ALU.add))
                settled()
                nc.vector.tensor_tensor(wc, wc, tp[2], ALU.add).then_inc(wconv_ok, 1)
            dve.wait_ge(dma_c, 160)
            dve.wait_ge(ident_ok, 8)
            step(nc.vector.tensor_copy(base[:, 0, :], firsts[:, :]))
            settled()

            def stats(src, st, m, n):
                for t in range(n):
                    step(nc.vector.bn_stats(st[:, t, :], src(t)))
                settled()
                for t in range(n):
                    step(nc.vector.bn_aggr(m[:, t, :], st[:, t, :]))
                settled()

            def rsqrt(y, var, eps, n):
                v, i, w = veps[:, 0:n], halved[:, 0:n], newton[:, 0:n]
                step(nc.vector.tensor_scalar(v, var, eps, None, ALU.add))
                settled()
                step(nc.vector.tensor_scalar(i, v.bitcast(I32), 1, None, ALU.logical_shift_right))
                settled()
                step(nc.vector.tensor_scalar(y.bitcast(I32), i, -1.0, float(0x5F3759DF), ALU.mult, ALU.add))
                settled()
                for _ in range(3):
                    step(nc.vector.tensor_tensor(w, y, y, ALU.mult))
                    settled()
                    step(nc.vector.scalar_tensor_tensor(out=w, in0=w, scalar=-0.5, in1=v, op0=ALU.mult, op1=ALU.mult))
                    settled()
                    step(nc.vector.scalar_tensor_tensor(out=y, in0=w, scalar=1.5, in1=y, op0=ALU.add, op1=ALU.mult))
                    settled()

            def patch_norm(q):
                dve.wait_ge(ytok_ok, q + 1)
                stats(lambda t: TOKM[:, t * P:(t + 1) * P], st6, mv, TPQ)
                rsqrt(rstd[:, :], mv[:, :, 1], TOK_EPS, TPQ)
                nc.vector.scalar_tensor_tensor(out=pshift[:, :], in0=mv[:, :, 0], scalar=-1.0, in1=rstd[:, :],
                                               op0=ALU.mult, op1=ALU.mult).then_inc(pstat_ok, 1)

            NH = NB * HEADS // 2

            def shift_scores(q):
                dve.wait_ge(sc_ps, q + 1)
                s3 = [SC[h][:, :].rearrange("p (a m) -> p a m", m=IMG) for h in range(2)]
                for h in range(2):
                    step(nc.vector.tensor_reduce(smax[:, h * NH:(h + 1) * NH], s3[h], AX.X, ALU.max))
                settled()
                for h in range(2):
                    last = nc.vector.tensor_tensor(
                        sc[:, h * NH:(h + 1) * NH, :], s3[h],
                        smax[:, h * NH:(h + 1) * NH].unsqueeze(2).to_broadcast([P, NH, IMG]), ALU.subtract)
                last.then_inc(sh_ok, 1)

            def normalize_probs(q):
                dve.wait_ge(exp_ok, q + 1)
                step(nc.vector.tensor_reduce(ssum[:, :], sc[:, :, :], AX.X, ALU.add))
                settled()
                step(nc.vector.reciprocal(srec[:, :], ssum[:, :]))
                settled()
                nc.vector.tensor_tensor(sc[:, :, :], sc[:, :, :],
                                        srec[:, :].unsqueeze(2).to_broadcast([P, NB * HEADS, IMG]),
                                        ALU.mult).then_inc(pn_ok, 1)

            def attention_norm(q):
                dve.wait_ge(att_ps, q + 1)
                nc.vector.tensor_tensor(res[:, :, :], ATT[:, :].rearrange("p (t d) -> p t d", d=D),
                                        dbrow[:, :].unsqueeze(1).to_broadcast([P, TPQ, D]),
                                        ALU.add).then_inc(res_ok, 1)
                dve.wait_ge(res_ok, q + 1)
                stats(lambda t: res[:, t, :], st6b, mvb, TPQ)
                rsqrt(rstdb[:, 0:TPQ], mvb[:, 0:TPQ, 1], LN_EPS, TPQ)
                nc.vector.scalar_tensor_tensor(out=shift[:, 0:TPQ], in0=mvb[:, 0:TPQ, 0], scalar=-1.0,
                                               in1=rstdb[:, 0:TPQ], op0=ALU.mult, op1=ALU.mult).then_inc(astat_ok, 1)
                if q == NQ - 1:
                    for t in range(2):
                        last = nc.vector.tensor_scalar(x1[:, q * TPQ + t, :], res[:, t, :], mvb[:, t, 0:1],
                                                       rstdb[:, t:t + 1], ALU.subtract, ALU.mult)
                    last.then_inc(x1_dve, 1)

            b4 = lambda a: a[:, :].unsqueeze(2).to_broadcast([P, R, 4])

            def router_logits(q):
                dve.wait_ge(lg_ps, q + 1)
                lv = LG[:, 0:TPQ * GR * 4].rearrange("p (t c) -> p t c", c=GR * 4)
                step(nc.vector.tensor_tensor(lg[:, :, :].rearrange("p (t g) e -> p t (g e)", g=GR), lv,
                                             br[:, :].unsqueeze(1).to_broadcast([P, TPQ, GR * 4]), ALU.add))
                settled()
                step(nc.vector.tensor_reduce(lmax[:, :], lg[:, :, :], AX.X, ALU.max))
                settled()
                nc.vector.tensor_tensor(lsh[:, :, :], lg[:, :, :], b4(lmax), ALU.subtract).then_inc(lsh_ok, 1)

            def router_weights(q):
                dve.wait_ge(lex_ok, q + 1)
                step(nc.vector.tensor_reduce(lsum[:, :], lex[:, :, :], AX.X, ALU.add))
                settled()
                step(nc.vector.reciprocal(lrec[:, :], lsum[:, :]))
                settled()
                step(nc.vector.tensor_tensor(gp[:, :, :], lex[:, :, :], b4(lrec), ALU.mult))
                settled()
                other = gp[:, :, :].unsqueeze(2).to_broadcast([P, R, 4, 4])
                own = gp[:, :, :].unsqueeze(3).to_broadcast([P, R, 4, 4])
                step(nc.vector.tensor_tensor(gt[:, :, :, :], other, own, ALU.is_gt))
                settled()
                for i in range(1, 4):
                    step(nc.vector.tensor_tensor(
                        gt[:, :, i, 0:i], gp[:, :, 0:i], gp[:, :, i:i + 1].to_broadcast([P, R, i]), ALU.is_ge))
                settled()
                step(nc.vector.tensor_reduce(rank[:, :, :], gt[:, :, :, :], AX.X, ALU.add))
                settled()
                step(nc.vector.tensor_scalar(top2[:, :, :], rank[:, :, :], 2.0, None, ALU.is_lt))
                step(nc.vector.tensor_scalar(first[:, :, :], rank[:, :, :], 0.0, None, ALU.is_equal))
                step(nc.vector.tensor_scalar(second[:, :, :], rank[:, :, :], 1.0, None, ALU.is_equal))
                settled()
                step(nc.vector.tensor_tensor(psec[:, :, :], gp[:, :, :], top2[:, :, :], ALU.mult))
                settled()
                step(nc.vector.tensor_reduce(cum[:, :], psec[:, :, :], AX.X, ALU.add))
                settled()
                step(nc.vector.tensor_scalar(keep2[:, :], cum[:, :], 0.9, None, ALU.is_le))
                settled()
                step(nc.vector.tensor_tensor(kept[:, :, :], second[:, :, :], b4(keep2), ALU.mult))
                settled()
                step(nc.vector.tensor_tensor(mask[:, :, :], first[:, :, :], kept[:, :, :], ALU.add))
                settled()
                step(nc.vector.tensor_tensor(mp[:, :, :], gp[:, :, :], mask[:, :, :], ALU.mult))
                settled()
                step(nc.vector.tensor_reduce(msum[:, :], mp[:, :, :], AX.X, ALU.add))
                settled()
                step(nc.vector.tensor_scalar(msum[:, :], msum[:, :], 1e-9, None, ALU.add))
                settled()
                step(nc.vector.reciprocal(mrec[:, :], msum[:, :]))
                settled()
                step(nc.vector.tensor_tensor(wn[:, :, :], mp[:, :, :], b4(mrec), ALU.mult))
                settled()
                wv = wn[:, :, :].rearrange("p (t g) e -> p t g e", g=GR)
                for t in range(TPQ):
                    step(nc.vector.scalar_tensor_tensor(
                        out=rows[:, q * TPQ + t, D:D + E].rearrange("p (g e) -> p g e", g=G),
                        in0=wv[:, t, 0, :].unsqueeze(2).to_broadcast([P, G, EPG]),
                        scalar=float(G ** -0.5), in1=wv[:, t, 1:GR, :], op0=ALU.mult, op1=ALU.mult))
                mk = mask[:, :, :].rearrange("p (t g) e -> p t g e", g=GR)
                fi = first[:, :, :].rearrange("p (t g) e -> p t g e", g=GR)
                ke = kept[:, :, :].rearrange("p (t g) e -> p t g e", g=GR)
                s4 = lambda a: a[:, :, :].rearrange("p t (g e) -> p t g e", g=G)
                over_e = lambda a: a[:, :, 0, :].unsqueeze(3).to_broadcast([P, TPQ, G, EPG])
                nc.vector.tensor_tensor(s4(sel), over_e(mk), mk[:, :, 1:GR, :], ALU.mult).then_inc(sel_ok, 1)
                for k, (a, b) in enumerate(((fi, fi), (fi, ke), (ke, fi), (ke, ke))):
                    step(nc.vector.tensor_tensor(s4(pick[:, k]), over_e(a), b[:, :, 1:GR, :], ALU.mult))
                settled()
                step(nc.vector.tensor_reduce(taken[:, :, :], pick[:, :, :, :], AX.X, ALU.add))

            def list_places(q):
                dve.wait_ge(count_ps, q + 1)
                t0 = q * TPQ
                for t in range(TPQ):
                    step(nc.vector.tensor_tensor(base[:, t0 + t + 1, :], base[:, t0 + t, :],
                                                 CNT[:, 64 + t * E:64 + (t + 1) * E], ALU.add))
                    settled()
                step(nc.vector.tensor_tensor(pos[:, :, :], CNT[:, 0:64].rearrange("p (t e) -> p t e", e=E),
                                             base[:, t0:t0 + TPQ, :], ALU.add))
                settled()
                te = lambda a: a[:, :, :, :].rearrange("p k t e -> p k (t e)")
                step(nc.vector.tensor_tensor(
                    te(picked), te(pick),
                    pos[:, :, :].rearrange("p t e -> p (t e)").unsqueeze(1).to_broadcast([P, K, TPQ * E]), ALU.mult))
                step(nc.vector.tensor_scalar(taken[:, :, :], taken[:, :, :], -float(SKIP), float(SKIP),
                                             ALU.mult, ALU.add))
                settled()
                step(nc.vector.tensor_reduce(place[:, :, :], picked[:, :, :, :], AX.X, ALU.add))
                settled()
                nc.vector.tensor_tensor(idx[:, q, :].rearrange("p (k t) -> p k t", k=K), place[:, :, :],
                                        taken[:, :, :], ALU.add).then_inc(idx_ok, 1)

            def table_column(first_tile, ends_of, count, less):
                step(nc.vector.tensor_scalar(past[:, :], ends_of, first_tile, None, ALU.is_le))
                settled()
                step(nc.vector.tensor_tensor(pastn[:, :], past[:, :], count, ALU.mult))
                step(nc.vector.tensor_reduce(tcol[:, 0:1], past[:, :], AX.X, ALU.add))
                settled()
                step(nc.vector.tensor_reduce(tcol[:, 1:2], pastn[:, :], AX.X, ALU.add))
                step(nc.vector.tensor_scalar(tcol[:, 2:3], tcol[:, 0:1], float(E - 1), None, ALU.min))
                step(nc.vector.tensor_scalar(tmp4[:, 0:1], tcol[:, 0:1], float(CAP), None, ALU.mult))
                settled()
                step(nc.vector.tensor_tensor(tmp4[:, 1:2], first_tile, tcol[:, 1:2], ALU.subtract))
                settled()
                if less is not None:
                    step(nc.vector.tensor_tensor(tmp4[:, 1:2], tmp4[:, 1:2], less, ALU.add))
                    settled()
                nc.vector.scalar_tensor_tensor(out=tcol[:, 3:4], in0=tmp4[:, 1:2], scalar=float(P), in1=tmp4[:, 0:1],
                                               op0=ALU.mult, op1=ALU.add).then_inc(tcol_ok, 1)

            def early_tiles():
                step(nc.vector.tensor_tensor(ntl[:, :], base[:, TILES - TPQ, :], firsts[:, :], ALU.subtract))
                settled()
                step(nc.vector.tensor_tensor(ngt[:, :, 0:TILES], ntl[:, :].unsqueeze(2).to_broadcast([P, E, TILES]),
                                             steps16[:, 1:].unsqueeze(1).to_broadcast([P, E, TILES]), ALU.is_ge))
                settled()
                step(nc.vector.tensor_reduce(full[:, :], ngt[:, :, 0:TILES], AX.X, ALU.add))
                settled()
                step(nc.vector.tensor_tensor_scan(ends[:, :], ones[:, 0:E], full[:, :], 0.0, ALU.mult, ALU.add))
                settled()
                table_column(tile_no[:, 0:1], ends[:, :], full[:, :], None)
                step(nc.vector.tensor_scalar(ends[:, :], ends[:, :], float(EARLY), None, ALU.min))
                step(nc.vector.memset(early[:, E:E + 1], 0.0))
                settled()
                step(nc.vector.tensor_copy(early[:, 0:1], ends[:, 0:1]))
                step(nc.vector.tensor_tensor(early[:, 1:E], ends[:, 1:E], ends[:, 0:E - 1], ALU.subtract))
                settled()
                step(nc.vector.tensor_tensor(early_step[:, :], early[:, 1:E + 1], early[:, 0:E], ALU.subtract))

            patch_norm(0)
            patch_norm(1)
            for q in range(NQ):
                shift_scores(q)
                if q and q + 1 < NQ:
                    patch_norm(q + 1)
                if q:
                    router_logits(q - 1)
                normalize_probs(q)
                if q:
                    router_weights(q - 1)
                    list_places(q - 1)
                if q == NQ - 1:
                    early_tiles()
                attention_norm(q)
            dve.wait_ge(trow_ps, 1)
            step(nc.vector.tensor_copy(expert_early[:, :], CNT[0:1, 0:EARLY]))
            step(nc.vector.tensor_scalar(place_early[:, :], CNT[0:1, P:P + EARLY], float(ROWS - P), None, ALU.min))
            settled()
            nc.vector.tensor_copy(tmp4[:, 2:3], tile_no[:, :]).then_inc(early_ok, 1)
            router_logits(NQ - 1)
            router_weights(NQ - 1)
            list_places(NQ - 1)
            nc.vector.tensor_copy(tail_row[:, :], base[0:1, TILES, :]).then_inc(tail_row_ok, 1)
            def put_xt(i, s):
                dve.wait_ge(xt_ps, i + 1)
                nc.vector.tensor_copy(xT[:, s, :], bank[7][:, 0:P]).then_inc(xt_ok, 1)

            def gated(i, s):
                dve.wait_ge(act_ok, i + 1)
                nc.vector.tensor_tensor(gu[:, s, :, :].rearrange("p c t -> p (c t)"), act[:, s, :],
                                        bank[2 * s + 1][:, :], ALU.mult).then_inc(gu_ok, 1)

            put_xt(0, 0)
            put_xt(1, 1)
            step(nc.vector.tensor_tensor(ntl[:, :], base[:, TILES, :], firsts[:, :], ALU.subtract))
            settled()
            step(nc.vector.tensor_tensor(ngt[:, :, :], ntl[:, :].unsqueeze(2).to_broadcast([P, E, TILES + 1]),
                                         steps16[:, :].unsqueeze(1).to_broadcast([P, E, TILES + 1]), ALU.is_gt))
            settled()
            step(nc.vector.tensor_reduce(ntl[:, :], ngt[:, :, :], AX.X, ALU.add))
            settled()
            step(nc.vector.tensor_tensor(ntl[:, :], ntl[:, :], early[:, 0:E], ALU.subtract))
            settled()
            step(nc.vector.tensor_tensor_scan(ends[:, :], ones[:, 0:E], ntl[:, :], 0.0, ALU.mult, ALU.add))
            step(nc.vector.tensor_tensor(full[:, :], ntl[:, :], early_step[:, :], ALU.subtract))
            settled()
            step(nc.vector.tensor_scalar(bodies_f[0:1, 0:1], ends[0:1, E - 1:E], 1 / U,
                                         EARLY / U - 0.5 - 0.5 / U,
                                         ALU.mult, ALU.add))
            table_column(late_no[:, 0:1], ends[:, :], full[:, :], early[:, 0:1])

            gated(0, 0)
            dve.wait_ge(up_ps, 1)
            put_xt(2, 0)
            gated(1, 1)
            dve.wait_ge(trow_ps, 2)
            step(nc.vector.tensor_copy(expert_row[:, :], CNT[0:1, 0:P]))
            step(nc.vector.tensor_scalar(place_row[:, :], CNT[0:1, P:2 * P], float(ROWS - P), None, ALU.min))
            step(nc.vector.tensor_copy(bodies_i[:, :], bodies_f[0:1, 0:1]))
            settled()
            step(nc.vector.tensor_copy(expert_row[:, 0:EARLY], expert_early[:, :]))
            settled()
            nc.vector.tensor_copy(tmp4[:, 2:3], tile_no[:, :]).then_inc(table_ok, 1)
            nc.vector.memset(tmp4[:, 3:4], 0.0).then_inc(yw_ok, 1)

            def results(j, experts, last=False):
                for u in range(U):
                    s = u % 2
                    i = j * U + (u + 1)
                    if not last or u + 3 < U:
                        dve.wait_ge(up_ps, i + 1)
                        put_xt(i + 2, 1 - s)
                    if not last or u + 2 < U:
                        dve.wait_ge(gut_ps, i)
                        gated(i + 1, s)
                    e = dve.value_load(experts[0:1, bass.ds(j * U + u, 1)], min_val=0, max_val=E - 1)
                    dve.wait_ge(y_ps, i)
                    dve.wait_ge(added[s], j * (8 * U) + (u // 2 * 16 + 16))
                    nc.vector.tensor_copy(ids[:, s:s + 1], meta[:, bass.ds((j * U + u) * META + E, 1)].bitcast(I32)
                                          ).then_inc(ids_ok, 1)
                    dve.wait_ge(ids_ok, i)
                    nc.vector.tensor_scalar(yw[:, s, :], bank[6][:, 0:D],
                                            meta[:, bass.ds((j * U + u) * META + e, 1)], None,
                                            ALU.mult).then_inc(yw_ok, 1)

            with dve.Fori(0, EARLY_STEPS // U) as j:
                results(j, expert_early)
            rest = dve.value_load(bodies_i[0:1, 0:1], min_val=MIN_BODIES - 1, max_val=MAX_BODIES - 1)
            with dve.Fori(EARLY_STEPS // U, rest) as j:
                results(j, expert_row)
            results(rest, expert_row, last=True)
            H = TILES // 2
            for h in range(2):
                dve.wait_ge(sums_in[h], 32)
                step(nc.vector.tensor_tensor(acc[:, 0, 4 * h:4 * h + 4, :], acc[:, 0, 4 * h:4 * h + 4, :],
                                             acc[:, 1, 4 * h:4 * h + 4, :], ALU.add))
            for h in range(4):
                if h < 2:
                    settled()
                else:
                    dve.wait_ge(summed[h - 2], 1)
                for t in range(4 * h, 4 * h + 4):
                    step(nc.vector.bn_stats(st6b[:, t, :], acc[:, 0, t, :]))
            settled()
            for t in range(TILES):
                step(nc.vector.bn_aggr(mvb[:, t, :], st6b[:, t, :]))
            settled()
            rsqrt(rstdb[:, :], mvb[:, :, 1], LN_EPS, TILES)
            nc.vector.scalar_tensor_tensor(out=shift[:, :], in0=mvb[:, :, 0], scalar=-1.0,
                                           in1=rstdb[:, :], op0=ALU.mult, op1=ALU.mult).then_inc(shift_ok, 1)
            for h in range(2):
                for t in range(h * H, h * H + LAST_DVE):
                    last = nc.vector.tensor_scalar(acc[:, 0, t, :], acc[:, 0, t, :], mvb[:, t, 0:1],
                                                   rstdb[:, t:t + 1], ALU.subtract, ALU.mult)
                last.then_inc(fin_ok, 1)

        @block.tensor
        def _(pe):
            T = nc.tensor

            def conv(q, chunks=range(CH)):
                s = q % 2
                if q:
                    pe.wait_ge(x_in[s], 32 * (q // 2 + 1))
                if q == 2:
                    pe.wait_ge(q_ok, 1)
                for ch in chunks:
                    k = P if ch < 6 else RIM
                    if q == 0 and ch == 0:
                        pe.wait_ge(wconv_ok, 1)
                        pe.wait_ge(x_first, 16)
                    if q == 0 and ch == 3:
                        pe.wait_ge(wconv_ok, 2)
                        pe.wait_ge(rim_in, 16)
                        pe.wait_ge(x_in[0], 32)
                    last = T.matmul(CONV[q][:, :], wconv[0:k, ch, :], xcol[0:k, s, ch, :],
                                    start=(ch == 0), stop=(ch == CH - 1))
                if ch == CH - 1:
                    last.then_inc(conv_ok, 1)

            def transposes(dst, src):
                for t in range(TPQ):
                    last = T.transpose(dst[:, t * P:(t + 1) * P], src(t), ident[:, :])
                return last

            tile = lambda a: (lambda t: a[:, t * P:(t + 1) * P])
            of_image = lambda a, i: a[:, :, :].rearrange("p h t -> p (h t)")[:, i:HEADS * QT:IPQ]
            held = ident[:, :].rearrange("p (c m) -> p c m", m=2 * IMG)[:, :, 0:IMG]
            b3 = lambda a: a.rearrange("p (c m) -> p c m", m=IMG)

            def keep_clock(n):
                for _ in range(n):
                    T.matmul(bank[0][:, 0:3 * D], ident[:, :], wqkv[:, :], start=True, stop=True)

            def tokens_out(q):
                pe.wait_ge(yct_ok, q + 1)
                if q > 1:
                    pe.wait_ge(res_ok, q - 1)
                transposes(TOKM, lambda t: ycT[:, q % 2, t * P:(t + 1) * P]).then_inc(ytok_ok, 1)

            def norm_back(q):
                pe.wait_ge(yn_ok, q + 1)
                if q > 1:
                    pe.wait_ge(lsh_ok, q - 1)
                transposes(NORM, lambda t: yn[:, t, :]).then_inc(ynt_ok, 1)

            def dense(q):
                pe.wait_ge(yt_ok, q + 1)
                T.matmul(H0T[:, :], dw[:, :], yT[:, q % 2, :], start=True, stop=True).then_inc(h0t_ps, 1)

            def residual(q):
                pe.wait_ge(yn_ok, min(q + 2, NQ))
                for t in range(TPQ):
                    T.matmul(ATT[:, t * P:(t + 1) * P], yT[:, q % 2, t * P:(t + 1) * P], dw[:, :],
                             start=(t == 0), stop=False)

            def keys(q):
                pe.wait_ge(h0t_ok, q + 1)
                T.matmul(KB[:, :], wqkv[:, D:2 * D], h0T[:, :], start=True, stop=True).then_inc(k_ps, 1)

            def values(q):
                T.matmul(VB[:, :], wqkv[:, 2 * D:3 * D], h0T[:, :], start=True, stop=True).then_inc(v_ps, 1)

            def queries(q):
                if 0 < q < NQ - 1:
                    pe.wait_ge(yct_ok, q + 2)
                T.matmul(QB[:, :], wqkv[:, 0:D], h0T[:, :], start=True, stop=True).then_inc(q_ps, 1)

            def scores(q):
                pe.wait_ge(kblk_in, 128 * (q + 1))
                pe.wait_ge(q_ok, q + 1)
                pe.wait_ge(v_ok, q + 1)
                pe.wait_ge(zeros, 4)
                for i in range(IPQ):
                    j, c = i // 4, i % 4
                    last = T.matmul(SC[j // 4][32 * c:32 * c + 32, (j % 4) * P:(j % 4 + 1) * P],
                                    qT[:, i * IMG:i * IMG + 32], kblk[:, :, i * IMG:(i + 1) * IMG],
                                    start=True, stop=True)
                last.then_inc(sc_ps, 1)

            def value_fills(q, fills):
                for f in fills:
                    if f == 0:
                        pe.wait_ge(vblk_in, 128 * (q + 1))
                    if f >= 2:
                        pe.wait_ge(vt_act, 8 * q + f - 1)
                    for i in range(4 * f, 4 * f + 4):
                        last = T.transpose(VT[f % 2][:, (i % 4) * D:(i % 4 + 1) * D],
                                           of_image(vblkT, i), ident[:, :])
                    last.then_inc(vt_ps, 1)

            def probs_back(q):
                pe.wait_ge(pn_ok, q + 1)
                for j in range(NB):
                    last = T.matmul(b3(PT[:, j * 64:(j + 1) * 64]),
                                    sc[:, j * HEADS:(j + 1) * HEADS, :].rearrange("p h m -> p (h m)"), held,
                                    start=True, stop=True)
                last.then_inc(pt_ps, 1)

            def context(q):
                pe.wait_ge(pt_ok, q + 1)
                pe.wait_ge(vt_act, 8 * q + 8)
                for i in range(IPQ):
                    j, c = i // 4, i % 4
                    last = T.matmul(CTX[j // 4][32 * c:32 * c + 32, (j % 4) * P:(j % 4 + 1) * P],
                                    pT[:, i * IMG:i * IMG + 32], vblk[:, i, :], start=True, stop=True)
                    if i % 16 == 15:
                        last.then_inc(ctx_ps, 1)

            def context_back(q):
                if q:
                    pe.wait_ge(lsh_ok, q)
                for j in range(NB):
                    pe.wait_ge(ctx_act, 2 * q + j // 4 + 1)
                    last = T.matmul(b3(CTXT[:, j * 64:(j + 1) * 64]), ctxs[:, j, :], held,
                                    start=True, stop=True)
                last.then_inc(ctxt_ps, 1)

            def attention_out(q):
                pe.wait_ge(ctx_ok, q + 1)
                for t in range(TPQ):
                    last = T.matmul(ATT[:, t * P:(t + 1) * P], ctxT[:, t * P:(t + 1) * P], wo[:, :],
                                    start=False, stop=(t == TPQ - 1))
                last.then_inc(att_ps, 1)

            def x1_turned(q):
                pe.wait_ge(x1_ok, q + 1)
                if q == NQ - 1:
                    pe.wait_ge(x1_dve, 1)
                if q:
                    pe.wait_ge(idx_ok, q)
                transposes(X1T, lambda t: x1[:, q * TPQ + t, :]).then_inc(x1t_ps, 1)

            def router(q):
                pe.wait_ge(x1t_ok, q + 1)
                for t in range(TPQ):
                    last = T.matmul(LG[:, t * GR * 4:(t + 1) * GR * 4], x1T[:, t * P:(t + 1) * P], wr[:, :],
                                    start=True, stop=True)
                last.then_inc(lg_ps, 1)

            def counts(q):
                pe.wait_ge(sel_ok, q + 1)
                pe.wait_ge(ident_ok, 8)
                selv = sel[:, :, :].rearrange("p t e -> p (t e)")
                T.matmul(CNT[:, 0:64], before[:, :], selv, start=True, stop=True)
                T.matmul(CNT[:, 64:128], ones[:, :], selv, start=True, stop=True).then_inc(count_ps, 1)

            def table_rows(n):
                pe.wait_ge(tcol_ok, n)
                T.matmul(CNT[0:1, 0:P], tcol[:, 2:3], ident[:, :], start=True, stop=True)
                T.matmul(CNT[0:1, P:2 * P], tcol[:, 3:4], ident[:, :], start=True, stop=True).then_inc(trow_ps, 1)

            pe.wait_ge(ident_ok, 1)
            conv(0)
            tokens_out(0)
            conv(1)
            pe.wait_ge(dma_c, 160)
            norm_back(0)
            tokens_out(1)
            dense(0)
            keys(0)
            values(0)
            queries(0)
            conv(2)
            for q in range(NQ):
                if q and q + 1 < NQ:
                    tokens_out(q + 1)
                scores(q)
                if q == 1:
                    conv(NQ - 1, range(0, 3))
                value_fills(q, (0, 1, 2, 3))
                if q:
                    keep_clock(1 if q > 1 else 0)
                    x1_turned(q - 1)
                if q == 1:
                    conv(NQ - 1, range(3, 5))
                value_fills(q, (4, 5))
                if q:
                    router(q - 1)
                value_fills(q, (6, 7))
                if q == 1:
                    conv(NQ - 1, range(5, 6))
                keep_clock((0, 0, 3, 5)[q])
                if q + 1 < NQ:
                    norm_back(q + 1)
                residual(q)
                if q == 1:
                    conv(NQ - 1, range(6, 7))
                if q + 1 < NQ:
                    dense(q + 1)
                if q == 1:
                    conv(NQ - 1, range(7, CH))
                probs_back(q)
                if q + 1 < NQ:
                    keys(q + 1)
                context(q)
                if q + 1 < NQ:
                    values(q + 1)
                if q:
                    counts(q - 1)
                context_back(q)
                attention_out(q)
                if q + 1 < NQ:
                    queries(q + 1)
            table_rows(1)
            keep_clock(8)
            pe.wait_ge(early_ok, 1)
            x1_turned(NQ - 1)
            router(NQ - 1)
            keep_clock(8)
            counts(NQ - 1)

            def x_transpose(i, s, loads):
                pe.wait_ge(xtile_in[s], loads)
                T.transpose(bank[7][:, 0:P], xin[:, s, :], ident[:, :]).then_inc(xt_ps, 1)

            def expert(i, experts):
                return pe.value_load(experts[0:1, bass.ds(i, 1)], min_val=0, max_val=E - 1)

            def up(i, s, e):
                pe.wait_ge(xt_ok, i + 1)
                T.matmul(bank[2 * s][:, :], xT[:, s, :], wall[:, bass.ds(e * WEXP, HID)], start=True, stop=True)
                T.matmul(bank[2 * s + 1][:, :], xT[:, s, :], wall[:, bass.ds(e * WEXP + HID, HID)],
                         start=True, stop=True).then_inc(up_ps, 1)

            def hidden_transpose(i, s):
                pe.wait_ge(gu_ok, i + 1)
                for c4 in range(HC):
                    last = T.transpose(bank[4 + s][:, c4 * P:(c4 + 1) * P], gu[:, s, c4, :], ident[:, :])
                last.then_inc(gut_ps, 1)

            def down(i, s, e):
                pe.wait_ge(gut_ok, i + 1)
                for c4 in range(HC):
                    last = T.matmul(bank[6][:, 0:D], guT[:, s, c4, :],
                                    wall[:, bass.ds(e * WEXP + 2 * HID + c4 * D, D)],
                                    start=(c4 == 0), stop=(c4 == HC - 1))
                last.then_inc(y_ps, 1)

            pe.wait_ge(early_ok, 1)
            pe.wait_ge(w_in, 16 * E)
            keep_clock(5)
            x_transpose(0, 0, 32)
            up(0, 0, expert(0, expert_early))
            x_transpose(1, 1, 32)
            up(1, 1, expert(1, expert_early))
            pe.wait_ge(xt_ok, 2)
            x_transpose(2, 0, 64)
            table_rows(2)
            hidden_transpose(0, 0)

            def steps(j, experts, last=False):
                for u in range(U):
                    s = u % 2
                    i = j * U + (u + 1)
                    e_up = expert(i + 1, experts) if not last or u + 2 < U else None
                    e_down = expert(i - 1, experts)
                    if e_up is not None:
                        pe.wait_ge(gu_ok, i)
                        up(i + 1, s, e_up)
                    if not last or u + 3 < U:
                        pe.wait_ge(xt_ok, i + 2)
                        x_transpose(i + 2, 1 - s, j * (16 * U) + (64 + 32 * ((u + 1) // 2)))
                    if not last or u + 1 < U:
                        hidden_transpose(i, 1 - s)
                    pe.wait_ge(yw_ok, i)
                    down(i - 1, s, e_down)

            with pe.Fori(0, EARLY_STEPS // U) as j:
                steps(j, expert_early)
            pe.wait_ge(table_ok, 1)
            rest = pe.value_load(bodies_i[0:1, 0:1], min_val=MIN_BODIES - 1, max_val=MAX_BODIES - 1)
            with pe.Fori(EARLY_STEPS // U, rest) as j:
                steps(j, expert_row)
            steps(rest, expert_row, last=True)


def host_layout(x, conv_w):
    import numpy as np
    x = np.asarray(x)
    w = np.asarray(conv_w)
    B = x.shape[0]
    S = 16
    xp = np.zeros((B, 66, 66, 3), x.dtype)
    xp[:, 1:65, 1:65] = x
    main = x.reshape(B, 4, S, 4, S, 3).transpose(2, 4, 5, 0, 1, 3).reshape(6, P, NQ, QT)
    main = np.ascontiguousarray(main.transpose(2, 1, 0, 3))
    cols = np.stack([xp[:, 1:65, 0:64:S], xp[:, 1:65, 17:66:S]])
    cols = cols.reshape(2, B, 4, S, 4, 3).transpose(0, 3, 5, 1, 2, 4).reshape(RIM, NQ, QT)
    rows = np.stack([xp[:, 0:64:S, 1:65], xp[:, 17:66:S, 1:65]])
    rows = rows.reshape(2, B, 4, 4, S, 3).transpose(0, 4, 5, 1, 2, 3).reshape(RIM, NQ, QT)
    rim = np.ascontiguousarray(np.stack([cols, rows]).transpose(2, 1, 0, 3))
    c, r, l, d, u = (w[:, :, 3 * i:3 * i + 3] for i in range(5))
    t = np.zeros((5, S, S, 3, D), w.dtype)
    t[0] = c
    t[1][:, :-1] = r[:, 1:]
    t[2][:, 1:] = l[:, :-1]
    t[3][:-1] = d[1:]
    t[4][1:] = u[:-1]
    taps = np.ascontiguousarray(t.reshape(5, 6, P, D).transpose(2, 0, 1, 3))
    wrim = np.stack([np.stack([r[:, 0], l[:, S - 1]]).reshape(RIM, D),
                     np.stack([d[0], u[S - 1]]).reshape(RIM, D)])
    return main, rim, taps, np.ascontiguousarray(wrim.transpose(1, 0, 2))


def kernel(**inputs):
    import numpy as np
    import concourse.bacc as bacc
    from concourse.bass_utils import run_bass_kernel_spmd

    g = {k: np.asarray(v) for k, v in inputs.items()}
    main, rim, taps, wrim = host_layout(g["x"], g["L0_tok_conv_w"])
    wroute = np.concatenate([g["L0_ffn_Wr"], g["L0_ffn_Wgate"].transpose(1, 0, 2).reshape(D, 16)], axis=1)
    broute = np.concatenate([g["L0_ffn_br"], g["L0_ffn_bgate"].reshape(16)])
    arrays = {
        "xmain": main, "xrim": rim, "taps": taps, "wrim": wrim,
        "conv_b": g["L0_tok_conv_b"], "gamma": g["L0_tok_gamma"], "beta": g["L0_tok_beta"],
        "dense_w": g["L0_tok_dense_w"], "dense_b": g["L0_tok_dense_b"],
        "wqkv_t": g["L0_attn_w_qkv"].T, "wo_t": g["L0_attn_w_o"].T,
        "wroute": wroute, "broute": broute,
        "wexp": np.concatenate([g["L0_ffn_W1"], g["L0_ffn_W3"],
                                g["L0_ffn_W2"].reshape(E, HC, P, D).transpose(0, 2, 1, 3).reshape(E, P, HC * D)],
                               axis=2),
    }
    arrays = {k: np.ascontiguousarray(v) for k, v in arrays.items()}
    nc = bacc.Bacc("TRN2", target_bir_lowering=False, num_devices=1)
    args = [nc.dram_tensor(f"in_{k}", v.shape, mybir.dt.from_np(v.dtype), kind="ExternalInput").ap()
            for k, v in arrays.items()]
    args.append(nc.dram_tensor("lists", (ROWS, ROW), F32, kind="Internal").ap())
    for name in ("sums_even", "sums_odd"):
        args.append(nc.dram_tensor(name, (TOKENS + P, D), F32, kind="Internal").ap())
    out = nc.dram_tensor("out", (P, TILES, D), F32, kind="ExternalOutput").ap()
    build_program(nc, *args, out)
    r = run_bass_kernel_spmd(nc, [{f"in_{k}": v for k, v in arrays.items()}], core_ids=[0])
    got = r.results[0]["out"]
    return np.ascontiguousarray(got.transpose(1, 0, 2)).reshape(NQ * IPQ, IMG, D)
```
